# Optimizing a Trainium2 kernel written in Bass

```python
import numpy as np
import jax
import jax.numpy as jnp

def _softmax(x, axis=-1):
    return jax.nn.softmax(x, axis=axis)

def _gelu(x):
    return jax.nn.gelu(x, approximate=True)

def _silu(x):
    return jax.nn.silu(x)

def _sigmoid(x):
    return jax.nn.sigmoid(x)

def _layernorm(x, axis=-1, eps=1e-05):
    m = jnp.mean(x, axis=axis, keepdims=True)
    v = jnp.var(x, axis=axis, keepdims=True)
    return (x - m) / jnp.sqrt(v + eps)

def _scatter_add(tgt, idx, src, axis=0):
    return tgt.at[idx].add(src)

def _segment_sum(src, seg, n):
    return jax.ops.segment_sum(src, seg, n)
kernel_name = 'mk_xattn_seq_d1_seqx_r4_9cd3ae'

def setup_inputs(seed: int=0):
    np.random.seed(seed)
    _w = jnp.asarray

    def _rec_inputs():
        import jax
        import jax.numpy as jnp
        _rk = jax.random.key(seed)
        x = 7.22e-05 + 1 * jax.random.normal(jax.random.fold_in(_rk, 1), (8, 256, 512), jnp.float32)
        _lenS = 256 - jax.random.randint(jax.random.fold_in(_rk, 7), (8,), 0, max(1, 256 // 4) + 1, jnp.int32)
        _lenS2 = 256 - jax.random.randint(jax.random.fold_in(_rk, 8), (8,), 0, max(1, 256 // 4) + 1, jnp.int32)
        _ctx_2048P = jax.random.normal(jax.random.fold_in(_rk, 11), (8, 16, 512), jnp.float32)
        _ctx_2048c = jax.random.dirichlet(jax.random.fold_in(_rk, 511), 0.3 * jnp.ones((16,), jnp.float32), (8, 256))
        _ctx_2048t = jnp.einsum('bsk,bkd->bsd', _ctx_2048c, _ctx_2048P)
        _ctx_2048t = _ctx_2048t * jax.lax.rsqrt(jnp.mean(jnp.square(_ctx_2048t)) + 1e-12) * 0.953939
        ctx_2048 = 2.81802e-05 + 1.00001 * (_ctx_2048t + 0.3 * jax.random.normal(jax.random.fold_in(_rk, 611), (8, 256, 512), jnp.float32))
        _validS = jnp.arange(256)[None, :] < _lenS[:, None]
        _validS2 = jnp.arange(256)[None, :] < _lenS2[:, None]
        _causal = jnp.tril(jnp.ones((256, 256), dtype=bool))
        mask_BxS2_bf1 = jnp.ones((8, 256), dtype=bool)
        return (x, ctx_2048, mask_BxS2_bf1)
    x, ctx_2048, mask_BxS2_bf1 = _rec_inputs()

    def _L0_xattn_setup():
        import jax, jax.numpy as jnp
        import numpy as np
        D = 512
        H = 16
        HD = D // H
        INNER = 4 * D
        EPS = 1e-05

        def layer_norm(x, w, b):
            mu = jnp.mean(x, axis=-1, keepdims=True)
            var = jnp.mean(jnp.square(x - mu), axis=-1, keepdims=True)
            return (x - mu) * jax.lax.rsqrt(var + EPS) * w + b
        key = jax.random.key(seed)
        ks = jax.random.split(key, 12)
        B, LQ, LK = (4, 256, 512)
        std = 0.02
        inp = {'hidden_states': jax.random.normal(ks[0], (B, LQ, D), jnp.float32), 'encoder_hidden_states': jax.random.normal(ks[1], (B, LK, D), jnp.float32), 'encoder_attention_mask': jnp.ones((B, LK), dtype=bool), 'ln1_w': jnp.ones((D,), jnp.float32), 'ln1_b': jnp.zeros((D,), jnp.float32), 'q_w': jax.random.normal(ks[2], (D, D), jnp.float32) * std, 'q_b': jnp.zeros((D,), jnp.float32), 'k_w': jax.random.normal(ks[3], (D, D), jnp.float32) * std, 'k_b': jnp.zeros((D,), jnp.float32), 'v_w': jax.random.normal(ks[4], (D, D), jnp.float32) * std, 'v_b': jnp.zeros((D,), jnp.float32), 'cproj_w': jax.random.normal(ks[5], (D, D), jnp.float32) * std, 'cproj_b': jnp.zeros((D,), jnp.float32), 'ln2_w': jnp.ones((D,), jnp.float32), 'ln2_b': jnp.zeros((D,), jnp.float32), 'fc_w': jax.random.normal(ks[6], (D, INNER), jnp.float32) * std, 'fc_b': jnp.zeros((INNER,), jnp.float32), 'proj_w': jax.random.normal(ks[7], (INNER, D), jnp.float32) * std, 'proj_b': jnp.zeros((D,), jnp.float32)}
        return inp
    _L0_xattn_all = _L0_xattn_setup()
    _L0_xattn_in = {k: v for k, v in _L0_xattn_all.items() if k in ('ln1_w', 'ln1_b', 'q_w', 'q_b', 'k_w', 'k_b', 'v_w', 'v_b', 'cproj_w', 'cproj_b', 'ln2_w', 'ln2_b', 'fc_w', 'fc_b', 'proj_w', 'proj_b')}
    del _L0_xattn_all
    return {'x': x, 'ctx_2048': ctx_2048, 'mask_BxS2_bf1': mask_BxS2_bf1, 'L0_xattn_ln1_w': _L0_xattn_in['ln1_w'], 'L0_xattn_ln1_b': _L0_xattn_in['ln1_b'], 'L0_xattn_q_w': _L0_xattn_in['q_w'], 'L0_xattn_q_b': _L0_xattn_in['q_b'], 'L0_xattn_k_w': _L0_xattn_in['k_w'], 'L0_xattn_k_b': _L0_xattn_in['k_b'], 'L0_xattn_v_w': _L0_xattn_in['v_w'], 'L0_xattn_v_b': _L0_xattn_in['v_b'], 'L0_xattn_cproj_w': _L0_xattn_in['cproj_w'], 'L0_xattn_cproj_b': _L0_xattn_in['cproj_b'], 'L0_xattn_ln2_w': _L0_xattn_in['ln2_w'], 'L0_xattn_ln2_b': _L0_xattn_in['ln2_b'], 'L0_xattn_fc_w': _L0_xattn_in['fc_w'], 'L0_xattn_fc_b': _L0_xattn_in['fc_b'], 'L0_xattn_proj_w': _L0_xattn_in['proj_w'], 'L0_xattn_proj_b': _L0_xattn_in['proj_b']}

def reference(x, ctx_2048, mask_BxS2_bf1, L0_xattn_ln1_w, L0_xattn_ln1_b, L0_xattn_q_w, L0_xattn_q_b, L0_xattn_k_w, L0_xattn_k_b, L0_xattn_v_w, L0_xattn_v_b, L0_xattn_cproj_w, L0_xattn_cproj_b, L0_xattn_ln2_w, L0_xattn_ln2_b, L0_xattn_fc_w, L0_xattn_fc_b, L0_xattn_proj_w, L0_xattn_proj_b):
    import jax
    import jax.numpy as jnp

    def _L0_xattn_ref(hidden_states, encoder_hidden_states, encoder_attention_mask, ln1_w, ln1_b, q_w, q_b, k_w, k_b, v_w, v_b, cproj_w, cproj_b, ln2_w, ln2_b, fc_w, fc_b, proj_w, proj_b):
        import jax, jax.numpy as jnp
        import numpy as np
        D = 512
        H = 16
        HD = D // H
        INNER = 4 * D
        EPS = 1e-05

        def layer_norm(x, w, b):
            mu = jnp.mean(x, axis=-1, keepdims=True)
            var = jnp.mean(jnp.square(x - mu), axis=-1, keepdims=True)
            return (x - mu) * jax.lax.rsqrt(var + EPS) * w + b
        B, LQ, _ = hidden_states.shape
        LK = encoder_hidden_states.shape[1]
        residual = hidden_states
        x = layer_norm(hidden_states, ln1_w, ln1_b)
        q = (x @ q_w + q_b).reshape(B, LQ, H, HD).transpose(0, 2, 1, 3)
        k = (encoder_hidden_states @ k_w + k_b).reshape(B, LK, H, HD).transpose(0, 2, 1, 3)
        v = (encoder_hidden_states @ v_w + v_b).reshape(B, LK, H, HD).transpose(0, 2, 1, 3)
        scale = 1.0 / np.sqrt(HD).astype(np.float32)
        scores = jnp.einsum('bhqd,bhkd->bhqk', q, k) * scale
        mask = encoder_attention_mask[:, None, None, :]
        mask_value = jnp.finfo(scores.dtype).min
        scores = jnp.where(mask, scores, mask_value)
        attn = jax.nn.softmax(scores, axis=-1)
        out = jnp.einsum('bhqk,bhkd->bhqd', attn, v)
        out = out.transpose(0, 2, 1, 3).reshape(B, LQ, D)
        out = out @ cproj_w + cproj_b
        hidden = out + residual
        residual = hidden
        y = layer_norm(hidden, ln2_w, ln2_b)
        y = jax.nn.gelu(y @ fc_w + fc_b, approximate=True)
        y = y @ proj_w + proj_b
        return residual + y
    x = _L0_xattn_ref(x, ctx_2048, mask_BxS2_bf1, L0_xattn_ln1_w, L0_xattn_ln1_b, L0_xattn_q_w, L0_xattn_q_b, L0_xattn_k_w, L0_xattn_k_b, L0_xattn_v_w, L0_xattn_v_b, L0_xattn_cproj_w, L0_xattn_cproj_b, L0_xattn_ln2_w, L0_xattn_ln2_b, L0_xattn_fc_w, L0_xattn_fc_b, L0_xattn_proj_w, L0_xattn_proj_b)
    return x

_drawn_inputs = setup_inputs


def setup_inputs(seed=0):
    import zlib

    import numpy as np

    out = dict(_drawn_inputs(seed))
    spreads = {'L0_xattn_ln1_w': (1.0, 0.6),
     'L0_xattn_ln1_b': (0.0, 0.8),
     'L0_xattn_q_b': (0.0, 0.8),
     'L0_xattn_k_b': (0.0, 0.8),
     'L0_xattn_v_b': (0.0, 0.1),
     'L0_xattn_cproj_b': (0.0, 0.1),
     'L0_xattn_ln2_w': (1.0, 0.2),
     'L0_xattn_ln2_b': (0.0, 0.342),
     'L0_xattn_fc_b': (0.0, 0.1),
     'L0_xattn_proj_b': (0.0, 0.1)}
    factors = {'L0_xattn_q_w': 7.266, 'L0_xattn_k_w': 7.116}
    for name, (base, spread) in spreads.items():
        noise = np.random.default_rng([zlib.crc32(name.encode()), seed]).standard_normal(out[name].shape)
        drawn = base * np.exp(spread * noise) if base else spread * noise
        out[name] = jnp.asarray(drawn.astype(out[name].dtype))
    for name, factor in factors.items():
        out[name] = (out[name] * factor).astype(out[name].dtype)
    return out
```

```python
import concourse.bass as bass
from concourse import mybir
from contextlib import ExitStack

fp32 = mybir.dt.float32
fp32r = mybir.dt.float32r
bf16 = mybir.dt.bfloat16
fp16 = mybir.dt.float16
u8 = mybir.dt.uint8
ALU = mybir.AluOpType
ACT = mybir.ActivationFunctionType
AX = mybir.AxisListType


def xattn_kernel(nc, x, ctx_in, mask, ln1_w, ln1_b, q_w, q_b, k_w, k_b, v_w, v_b, c_w, c_b,
                 ln2_w, ln2_b, fc_w, fc_b, proj_w, proj_b, out):
    B, LQ, D = x.shape
    LK = ctx_in.shape[1]
    H, HD = 16, 32
    INNER = fc_w.shape[1]
    P = 128
    KT = D // P
    TT = LQ // P
    KC = LK // P
    GH = P // HD
    NG = H // GH
    GROUPS = B * NG
    FT = INNER // P
    CH = 4
    CW = CH * P
    CHUNKS = B * LQ // CW
    VW = 1 + 3 * HD
    VW_LO = 1 + 2 * HD
    SCALE = float(HD) ** -0.5
    EPS = 1e-5
    PSHIFT = 7.5
    MASKED = float(2.0 ** 127)
    MAXROWS = 3 * HD + 1
    SUBROWS = 3 * HD + 3
    SCALE32 = float(mybir_f32(SCALE))

    ctx = ExitStack()
    with ctx:
        def sb(name, shape, dt, offset):
            return nc.alloc_sbuf_tensor_at(name, shape, dt, offset=offset)

        BASE = 16512
        KB = 1024
        hidden = sb("hidden", [P, B * TT, D], fp32, BASE)
        C0 = BASE + 32 * KB
        ident = sb("ident", [P, P], fp32, C0)
        cols = sb("cols", [P, 6 * KT + FT], fp32, C0 + 512)
        maskcol = sb("maskcol", [P, B * KC], fp32, C0 + 704)
        maskcol_raw = sb("maskcol_raw", [P, B * KC], u8, C0 + 768)
        stats = sb("stats", [P, 2, 6], fp32, C0 + 800)
        mv = sb("mv", [P, 2, 2], fp32, C0 + 864)
        rstd = sb("rstd", [P, 2], fp32, C0 + 896)
        mhalf = sb("mhalf", [P, 2], fp32, C0 + 928)
        vareps = sb("vareps", [P, 2], fp32, C0 + 960)
        maskbias = sb("maskbias", [P, KC], fp32, C0 + 992)
        scratch = sb("scratch", [P, 1], fp32, C0 + 1024)
        R0 = C0 + 1056

        w_att = sb("w_att", [P, 4, 2, KT, D], fp32r, R0)
        w_att_raw = sb("w_att_raw", [P, 4, 2, KT, D], fp32, R0)
        A1 = R0 + 64 * KB
        stacks = sb("stacks", [P, 2, H, LQ], fp32r, A1)
        qst, kst = stacks[:, 0], stacks[:, 1]
        A2 = A1 + 32 * KB
        att_t = sb("att_t", [P, 2, KT, LQ], fp32r, A2)
        xc_t = sb("xc_t", [P, 2, KT, LQ], fp32, A2)
        p32 = sb("p32", [P, 2, 2 * LQ], fp32, A2 + 8 * KB)
        p_hi = sb("p_hi", [P, 8, 2 * LQ], fp16, A2 + 12 * KB)
        p_lo = sb("p_lo", [P, 8, 2 * LQ], fp16, A2 + 20 * KB)
        vparts = sb("vparts", [P, KC, H, VW], bf16, A2 + 28 * KB)
        A3 = R0 + 131 * KB
        xs = sb("xs", [P, 2, KT, LQ], fp32r, A3)
        cs = sb("cs", [P, 2, KT, LK], fp32r, A3 + 8 * KB)
        ctx_sb = sb("ctx_sb", [P, KC, D], fp32, A3 + 16 * KB)
        xn = sb("xn", [P, TT, D], fp32, A3 + 20 * KB)
        qk = sb("qk", [P, 4, LQ], fp32r, A3 + 24 * KB)
        v32 = sb("v32", [P, KC, D], fp32, A3 + 28 * KB)
        A4 = A3 + 32 * KB
        att = sb("att", [P, TT, D], fp32, A4)
        vb_bc = sb("vb_bc", [P, D], fp32, A4 + 4 * KB)
        cb_bc = sb("cb_bc", [P, D], fp32, A4 + 6 * KB)
        A5 = A4 + 8 * KB
        negm = sb("negm", [P, TT, GH], fp32, A5)
        m12 = sb("m12", [P, TT, 3 * GH], fp32r, A5 + 32)
        rl = sb("rl", [P, TT, H], fp32, A5 + 160)
        mrow = sb("mrow", [3 * GH, LQ], fp32r, A5 + 288)
        ones_row = sb("ones_row", [1, LQ], fp32, A5 + 288 + KB)
        mrow_raw = sb("maskrow_raw", [B, LK], u8, A5 + 288 + 2 * KB)
        maskrow = sb("maskrow", [B, LK], fp32, A5 + 544 + 2 * KB)
        w_mlp = [sb(f"w_mlp{i}", [P, 4, D], fp32r, R0 + 8 * KB * i) for i in range(FT)]
        w_mlp_raw = [sb(f"w_mlp_raw{i}", [P, 4, D], fp32, R0 + 8 * KB * i) for i in range(FT)]
        y_hi = sb("y_hi", [P, KT, CW], fp32r, A3)
        y_lo = sb("y_lo", [P, KT, CW], fp32r, A3 + 8 * KB)
        yn = sb("yn", [P, 2, D], fp32, A3 + 16 * KB)
        y_t = sb("y_t", [P, KT, CW], fp32, A3 + 20 * KB)
        h32 = sb("h32", [P, 2, CW], fp32, A3 + 28 * KB)
        h_hi = sb("h_hi", [P, 2, CW], fp32r, A3 + 32 * KB)
        h_lo = sb("h_lo", [P, 2, CW], fp32r, A3 + 36 * KB)
        pb_bc = sb("pb_bc", [P, D], fp32, A3 + 40 * KB)
        assert A3 + 42 * KB <= 229344 and A5 + 544 + 3 * KB <= 229344

        mask_rows = nc.dram_tensor("mask_rows", [B, LK], fp32, kind="Internal").ap()

        LN1W, LN1B, QB, KB_, LN2W, LN2B, FCB = [KT * i for i in range(7)]

        psum = ctx.enter_context(nc.psum_tensor("psum", [P, 8, 512], fp32))
        ST, MX, PV, MS = 0, 2, 4, 6
        ACC, TR, FC = 0, 4, 6

        names = """x_loaded ctx_loaded small_loaded mask_stored out_stored
            ident_zero ident_ready pool_consts zeros_ready mask_ready maskbias_ready
            wq_loaded wk_loaded wv_loaded wc_loaded w_hi_dve w_hi_act w_lo_dve w_lo_pool
            qk_proj x_tr ctx_tr max_mm st_mm pv_mm m_tr att_tr v_proj c_proj
            x_affine ctx_copied qk_hi_done qk_lo_done p_hi_done p_lo_done mrow_ready att_hi_done att_lo_done
            v_cast v_rest v_split v_added max_taken m_hi_done m_lo_done pv_taken att_normed hidden_added
            ln_stats ln_mv ln_var ln_rstd x_normed cb_added split_hi split_lo
            stack_filled0 stack_filled1 m_stored
            w2_hi w2_lo fc_mm proj_mm y_tr y_affine y_normed y_hi_done y_lo_done h_done h_hi_done h_lo_done
            pb_loaded pb_added out_added y_stats y_mv y_var y_rstd""".split()
        s = {n: ctx.enter_context(nc.semaphore(n)) for n in names}
        w2_loaded = [ctx.enter_context(nc.semaphore(f"w2_loaded{i}")) for i in range(FT)]
        stack_filled = [s["stack_filled0"], s["stack_filled1"]]
        FILLS = (3 * GH + 2) * 16

        def wait(eng, sem, value):
            if not isinstance(value, int) or value > 0:
                eng.wait_ge(s[sem] if isinstance(sem, str) else sem, value)

        def batch(b):
            return not isinstance(b, int) or 0 <= b < B

        def group(G):
            return not isinstance(G, int) or 0 <= G < GROUPS

        USES = [("qk", 0), ("m", 0),
                ("qk", 1), ("v", 0), ("att", 0), ("att", 1), ("m", 1),
                ("qk", 2), ("v", 1), ("c", 0), ("m", 2),
                ("qk", 3), ("c", 1), ("x", 0), ("x", 1), ("ctx", 0), ("ctx", 1), ("m", 3)]

        def emptied(it, kind, n):
            if kind in ("qk", "m"):
                G = it * NG + n + (3 if kind == "qk" else 2)
                if not group(G):
                    return None
                return ("qk_lo_done", (G + 1) * 2) if kind == "qk" else ("mrow_ready", G + 1)
            b = it + {"v": 1, "att": -1, "c": -1, "x": 2, "ctx": 2}[kind]
            if not batch(b):
                return None
            return {"v": ("v_added", b * 2 + (n + 1)), "att": ("att_lo_done", b * 2 + (n + 1)),
                    "c": ("hidden_added", b * 2 + (n + 1)), "x": ("x_affine", b * 4 + 2 * (n + 1)),
                    "ctx": ("ctx_copied", b * 2 + (n + 1))}[kind]

        def bank_of(it, kind, n):
            k = USES.index((kind, n))
            for back in range(k - 2, k - 2 - 2 * len(USES), -2):
                before = emptied(it + back // len(USES), *USES[back % len(USES)])
                if before:
                    wait(nc.tensor, *before)
                    break
            return psum[:, MS + k % 2, :]

        def in_bank(kind, n):
            return psum[:, MS + USES.index((kind, n)) % 2, :]

        def iterations(eng, step):
            for it in (-2, -1, 0):
                for g in range(NG):
                    step(it, g)
            with eng.Fori(1, B - 2) as it:
                for g in range(NG):
                    step(it, g)
            for it in (B - 2, B - 1, B):
                for g in range(NG):
                    step(it, g)

        def chunks(eng, body):
            body(0, True)
            with eng.Fori(1, CHUNKS - 1) as c:
                body(c, False)
            body(CHUNKS - 1, False)

        def has_next(c):
            return not isinstance(c, int) or c < CHUNKS - 1

        def hidden_tile(j):
            if isinstance(j, int):
                return hidden[:, j, :]
            return hidden[:, bass.ds(j, 1), :].rearrange("p o d -> p (o d)")

        def min_batch(n):
            return min(n + 1, B) if isinstance(n, int) else n + 1

        def fills_upto(G, parity):
            if isinstance(G, int):
                return (G // 2 + 1) * FILLS if G >= 0 else 0
            return (G - parity) * (FILLS // 2) + FILLS

        block = ctx.enter_context(nc.Block())

        @block.sync
        def _(sp):
            def address_follows():
                sp.wait_ge(s["pool_consts"], 1)

            def load_tokens(b):
                wait(sp, "x_loaded", b * 16)
                address_follows()
                sp.dma_start(hidden[:, bass.ds(b * TT, TT), :] if not isinstance(b, int) else hidden[:, b * TT:(b + 1) * TT, :],
                             x_rows(x, b)).then_inc(s["x_loaded"], 16)
                wait(sp, "ctx_tr", b * 2)
                address_follows()
                sp.dma_start(ctx_sb[:, :, :], x_rows(ctx_in, b)).then_inc(s["ctx_loaded"], 16)

            def x_rows(src, b):
                rows = src[b:b + 1] if isinstance(b, int) else src[bass.ds(b, 1)]
                return rows.rearrange("o (t p) d -> p (o t) d", p=P)

            load_tokens(0)
            for n, (w, sem) in enumerate(((q_w, "wq_loaded"), (k_w, "wk_loaded"), (v_w, "wv_loaded"), (c_w, "wc_loaded"))):
                sp.dma_start(w_att_raw[:, n, 1, :, :], w.rearrange("(k p) n -> p k n", p=P)).then_inc(s[sem], 16)
            sp.wait_ge(s["mask_ready"], 2)
            sp.dma_start(mask_rows, maskrow[:, :]).then_inc(s["mask_stored"], 16)
            sp.wait_ge(s["mask_stored"], 16)
            sp.wait_ge(s["pool_consts"], 5)

            def step(it, g):
                G = it * NG + g + 3
                b = it if g == 0 else it + 1
                if g == 0 and batch(it + 2) and not (isinstance(it, int) and it == -2):
                    load_tokens(it + 2)
                if group(G):
                    slot = slice(GH * ((g + 3) % NG), GH * ((g + 3) % NG) + GH)
                    filled = stack_filled[(g + 3) % 2]
                    wait(sp, "qk_lo_done", (G + 1) * 2)

                    def fill(dst, src):
                        sp.dma_start(dst, src).then_inc(filled, 16)

                    for h in range(GH):
                        rows = slice(HD * h, HD * h + HD)
                        for r, parts in enumerate((slice(1, 3), slice(1, 4, 2), slice(0, 3, 2))):
                            fill(stacks[HD * r:HD * r + HD, :, slot.start + h, :].bitcast(fp32), qk[rows, parts, :].bitcast(fp32))
                    fill(qst[3 * HD:3 * HD + 1, slot, :].bitcast(fp32),
                         ones_row[0:1, :].rearrange("p (o q) -> p o q", o=1).to_broadcast([1, GH, LQ]))
                    row = mask_rows[b:b + 1, :] if isinstance(b, int) else mask_rows[bass.ds(b, 1), :]
                    fill(kst[3 * HD:3 * HD + 1, slot, :].bitcast(fp32),
                         row.rearrange("p (o q) -> p o q", o=1).to_broadcast([1, GH, LK]))
                G = it * NG + g + 2
                if group(G):
                    slot = slice(GH * ((g + 2) % NG), GH * ((g + 2) % NG) + GH)
                    wait(sp, "mrow_ready", G + 1)
                    for j in range(3):
                        sp.dma_start(qst[3 * HD + j:3 * HD + j + 1, slot, :].bitcast(fp32),
                                     mrow[j * GH:(j + 1) * GH, :].bitcast(fp32)).then_inc(s["m_stored"], 16)
            iterations(sp, step)

            for i in range(FT):
                if i == 0:
                    wait(sp, "qk_proj", GROUPS)
                    wait(sp, "v_proj", B * 2)
                if i == 6:
                    wait(sp, "c_proj", B * 2)
                sp.dma_start(w_mlp_raw[i][:, 1, :].rearrange("p (k f) -> p k f", k=KT),
                             fc_w[:, i * P:(i + 1) * P].rearrange("(k p) f -> p k f", p=P)).then_inc(w2_loaded[i], 16)
                sp.dma_start(w_mlp_raw[i][:, 3, :], proj_w[i * P:(i + 1) * P, :]).then_inc(w2_loaded[i], 16)
                if i == 6:
                    sp.dma_start(pb_bc[:, :], proj_b.rearrange("(o n) -> o n", o=1).to_broadcast([P, D])).then_inc(s["pb_loaded"], 16)

            def store(c, first):
                for t in range(CH):
                    wait(sp, "out_added", c * CH + (t + 1))
                    address_follows()
                    rows = out_rows(c * CH + t)
                    src = hidden[:, c * CH + t, :] if isinstance(c, int) else hidden[:, bass.ds(c * CH + t, 1), :].rearrange("p o d -> p (o d)")
                    sp.dma_start(rows, src).then_inc(s["out_stored"], 16)

            def out_rows(j):
                flat = out.rearrange("b (t p) d -> (b t) p d", p=P)
                return flat[j] if isinstance(j, int) else flat[bass.ds(j, 1)].rearrange("o p d -> (o p) d")

            chunks(sp, store)
            sp.wait_ge(s["out_stored"], 16 * B * TT)

        @block.gpsimd
        def _(pool):
            for dst, src in ((cols[:, LN1W:LN1W + KT], ln1_w), (cols[:, LN1B:LN1B + KT], ln1_b),
                             (cols[:, QB:QB + KT], q_b), (cols[:, KB_:KB_ + KT], k_b),
                             (cols[:, LN2W:LN2W + KT], ln2_w), (cols[:, LN2B:LN2B + KT], ln2_b),
                             (cols[:, FCB:FCB + FT], fc_b)):
                with nc.allow_non_contiguous_dma(reason="per-partition vectors, a few KB"):
                    pool.dma_start(dst, src.rearrange("(k p) -> p k", p=P)).then_inc(s["small_loaded"], 16)
            with nc.allow_non_contiguous_dma(reason="the mask's columns, 2 KB"):
                pool.dma_start(maskcol_raw[:, :], mask.rearrange("b (c p) -> p (b c)", p=P)).then_inc(s["small_loaded"], 16)
            pool.dma_start(mrow_raw[:, :], mask).then_inc(s["small_loaded"], 16)
            pool.dma_start(vb_bc[:, :], v_b.rearrange("(o n) -> o n", o=1).to_broadcast([P, D])).then_inc(s["small_loaded"], 16)
            pool.dma_start(cb_bc[:, :], c_b.rearrange("(o n) -> o n", o=1).to_broadcast([P, D])).then_inc(s["small_loaded"], 16)
            pool.memset(ident[:, :], 0.0).then_inc(s["ident_zero"], 1)
            pool.wait_ge(s["ident_zero"], 1)
            pool.affine_select(out=ident[:, :], in_=ident[:, :], compare_op=ALU.not_equal, fill=1.0,
                               base=0, pattern=[[-1, P]], channel_multiplier=1).then_inc(s["ident_ready"], 1)
            pool.memset(mhalf[:, :], -0.5).then_inc(s["pool_consts"], 1)
            pool.memset(m12[:, :, :].bitcast(fp32), 0.0).then_inc(s["pool_consts"], 1)
            pool.memset(vparts[:, :, :, 0:1], 1.0).then_inc(s["pool_consts"], 1)
            pool.memset(ones_row[:, :], 1.0).then_inc(s["pool_consts"], 1)
            pool.wait_ge(s["pool_consts"], 4)
            pool.memset(kst[3 * HD:3 * HD + 3, :, :].bitcast(fp32), 1.0).then_inc(s["pool_consts"], 1)
            pool.wait_ge(s["pool_consts"], 5)

            def inverse_std(b, n, var_sem, out_sem):
                wait(pool, var_sem, b + 1)
                pool.tensor_tensor(rstd[:, 0:n], vareps[:, 0:n], mhalf[:, 0:n], ALU.pow).then_inc(s[out_sem], 1)

            def split_weight_lo(n, loaded):
                pool.wait_ge(s["w_hi_act"], n - 1)
                pool.tensor_tensor(w_att[:, n, 1, :, :], w_att_raw[:, n, 1, :, :], w_att[:, n, 0, :, :].bitcast(fp32),
                                   ALU.subtract).then_inc(s["w_lo_pool"], 1)

            def step(it, g):
                if g == 1 and batch(it - 1):
                    b = it - 1
                    wait(pool, "pv_taken", (b + 1) * 16)
                    for t in range(TT):
                        a = att[:, t, :].rearrange("p (h d) -> p h d", h=H)
                        pool.tensor_tensor(a, a, rl[:, t, :].rearrange("p (h o) -> p h o", o=1).to_broadcast([P, H, HD]),
                                           ALU.mult).then_inc(s["att_normed"], 1)
                if isinstance(it, int) and it == -2 and g == 1:
                    inverse_std(0, TT, "ln_var", "ln_rstd")
                    split_weight_lo(2, "wv_loaded")
                    split_weight_lo(3, "wc_loaded")
                G = it * NG + g
                if group(G):
                    for u in range(4):
                        wait(pool, "p_hi_done", (G * 4) + (u + 1))
                        wait(pool, "pv_mm", (G - 1) * 2)
                        slot = (g % 2) * 4 + u
                        pool.tensor_tensor(p_lo[:, slot, :], p32[:, u % 2, :], p_hi[:, slot, :],
                                           ALU.subtract).then_inc(s["p_lo_done"], 1)
                if g == 1 and batch(it + 2) and not (isinstance(it, int) and it == -2):
                    inverse_std(it + 2, TT, "ln_var", "ln_rstd")
                if g == 3 and batch(it + 2):
                    b = it + 2
                    wait(pool, "x_normed", (b + 1) * 2)
                    wait(pool, "small_loaded", 11 * 16)
                    for t in range(TT):
                        h = hidden_tile(b * TT + t)
                        pool.tensor_tensor(h, h, cb_bc[:, :], ALU.add).then_inc(s["cb_added"], 1)

            iterations(pool, step)

            def ln2(j):
                inverse_std(j, 1, "y_var", "y_rstd")

            def pb(j):
                wait(pool, "y_normed", j + 1)
                h = hidden_tile(j)
                pool.tensor_tensor(h, h, pb_bc[:, :], ALU.add).then_inc(s["pb_added"], 1)

            for t in range(CH):
                ln2(t)
            pool.wait_ge(s["pb_loaded"], 16)
            for t in range(CH):
                pb(t)

            def body(c, first):
                if has_next(c):
                    for t in range(CH):
                        ln2(c * CH + (CH + t))
                        pb(c * CH + (CH + t))

            chunks(pool, body)

        @block.scalar
        def _(act):
            for n, sem in ((2, "wv_loaded"), (3, "wc_loaded")):
                act.wait_ge(s[sem], 16)
                act.activation(w_att[:, n, 0, :, :], w_att_raw[:, n, 1, :, :], ACT.Copy).then_inc(s["w_hi_act"], 1)
            act.wait_ge(s["small_loaded"], 11 * 16)
            act.wait_ge(s["mask_ready"], 3)

            def exps(it, g, pair):
                G = it * NG + g
                if not group(G):
                    return
                for kc in range(KC):
                    u = 2 * pair + kc
                    n = G * 4 + u
                    wait(act, "st_mm", n + 1)
                    wait(act, "p_lo_done", n - 1)
                    act.activation(p32[:, u % 2, :], psum[:, ST + kc, :], ACT.Exp, bias=maskbias[:, kc:kc + 1], scale=SCALE32)
                    wait(act, "pv_mm", (G - 1) * 2)
                    act.activation(p_hi[:, (g % 2) * 4 + u, :], psum[:, ST + kc, :], ACT.Exp, bias=maskbias[:, kc:kc + 1],
                                   scale=SCALE32).then_inc(s["p_hi_done"], 1)

            def values_cast(b, part):
                wait(act, "v_added", (b + 1) * 2)
                wait(act, "pv_mm", b * 8)
                if part:
                    wait(act, "v_rest", b + 1)
                lo = 1 + HD * part
                act.activation(vparts[:, :, :, lo:lo + HD], v32[:, :, :].rearrange("p c (h d) -> p c h d", h=H),
                               ACT.Copy).then_inc(s["v_cast"], 1)

            def step(it, g):
                if g == 0 and batch(it):
                    wait(act, "maskbias_ready", it + 1)
                if g == 1 and batch(it):
                    values_cast(it, 0)
                exps(it, g, 0)
                if g == 1 and batch(it):
                    values_cast(it, 1)
                G = it * NG + g + 3
                if group(G):
                    wait(act, "qk_proj", G + 1)
                    prior = stack_filled[(g + 2) % 2]
                    wait(act, prior, fills_upto(G - 1, (g + 2) % 2))
                    for n, col in ((0, QB), (1, KB_)):
                        act.activation(qk[:, 1 + n, :], in_bank("qk", g)[:, n * LQ:(n + 1) * LQ], ACT.Identity,
                                       bias=cols[:, col + (g + 3) % NG:col + (g + 3) % NG + 1]).then_inc(s["qk_hi_done"], 1)
                exps(it, g, 1)
                if g == 1 and batch(it - 1):
                    b = it - 1
                    wait(act, "split_lo", min_batch(it + 1) * 2)
                    wait(act, "c_proj", b * 2)
                    for j in range(2):
                        wait(act, "att_tr", b * 2 + (j + 1))
                        act.activation(att_t[:, 0, 2 * j:2 * j + 2, :], in_bank("att", j).rearrange("p (k q) -> p k q", k=2),
                                       ACT.Copy).then_inc(s["att_hi_done"], 1)
                if g == 3 and batch(it + 2):
                    b = it + 2
                    wait(act, "split_lo", b * 2)
                    wait(act, "c_proj", it * 2)
                    for j in range(2):
                        wait(act, "x_tr", b * 2 + (j + 1))
                        for i in range(2):
                            k = 2 * j + i
                            act.activation(xc_t[:, 0, k, :], in_bank("x", j)[:, i * LQ:(i + 1) * LQ], ACT.Identity,
                                           scale=cols[:, LN1W + k:LN1W + k + 1],
                                           bias=cols[:, LN1B + k:LN1B + k + 1]).then_inc(s["x_affine"], 1)
                    for j in range(2):
                        wait(act, "ctx_tr", b * 2 + (j + 1))
                        act.activation(xc_t[:, 1, 2 * j:2 * j + 2, :], in_bank("ctx", j).rearrange("p (k q) -> p k q", k=2),
                                       ACT.Copy).then_inc(s["ctx_copied"], 1)
                G = it * NG + g + 2
                if g == 3 and batch(it + 1):
                    wait(act, "p_hi_done", (it + 1) * 16)
                if group(G):
                    wait(act, "m_tr", G + 1)
                    wait(act, "m_stored", G * 48)
                    act.activation(mrow[:, :], in_bank("m", g)[0:3 * GH, 0:LQ], ACT.Copy).then_inc(s["mrow_ready"], 1)
                if g == 3 and batch(it + 1):
                    b = it + 1
                    cut = slice(b * KC, (b + 1) * KC) if isinstance(it, int) else bass.ds(b * KC, KC)
                    act.activation(maskbias[:, :], maskcol[:, cut], ACT.Copy).then_inc(s["maskbias_ready"], 1)

            iterations(act, step)

            def affine(j, t):
                wait(act, "y_tr", j + 1)
                wait(act, "y_lo_done", (j - t))
                for k in range(KT):
                    act.activation(y_t[:, k, t * P:(t + 1) * P], psum[:, TR + t % 2, k * P:(k + 1) * P], ACT.Identity,
                                   scale=cols[:, LN2W + k:LN2W + k + 1],
                                   bias=cols[:, LN2B + k:LN2B + k + 1]).then_inc(s["y_affine"], 1)

            def gelu(F, f):
                wait(act, "fc_mm", F + 1)
                wait(act, "h_lo_done", F - 1)
                act.activation(h32[:, f % 2, :], psum[:, FC + f % 2, :], ACT.Gelu_apprx_tanh,
                               bias=cols[:, FCB + f:FCB + f + 1]).then_inc(s["h_done"], 1)

            for t in range(CH):
                affine(t, t)
            gelu(0, 0)

            def body(c, first):
                for i in range(FT):
                    if i < FT - 1:
                        gelu(c * FT + (i + 1), i + 1)
                    elif has_next(c):
                        gelu(c * FT + FT, 0)
                    if has_next(c) and i % 3 == 0 and 3 <= i <= 12:
                        t = i // 3 - 1
                        affine(c * CH + (CH + t), t)

            chunks(act, body)

        @block.vector
        def _(dve):
            for n, sem in ((0, "wq_loaded"), (1, "wk_loaded")):
                dve.wait_ge(s[sem], 16)
                dve.tensor_copy(w_att[:, n, 0, :, :], w_att_raw[:, n, 1, :, :]).then_inc(s["w_hi_dve"], 1)
            dve.wait_ge(s["small_loaded"], 11 * 16)
            dve.tensor_scalar(maskrow[:, :], mrow_raw[:, :], MASKED, -MASKED, ALU.mult, ALU.add).then_inc(s["mask_ready"], 1)
            dve.tensor_scalar(maskcol[:, :], maskcol_raw[:, :], SCALE32 * MASKED, -SCALE32 * MASKED,
                              ALU.mult, ALU.add).then_inc(s["mask_ready"], 1)
            dve.wait_ge(s["mask_ready"], 2)
            dve.tensor_scalar_add(maskcol[:, :], maskcol[:, :], PSHIFT).then_inc(s["mask_ready"], 1)
            for n in range(2):
                dve.wait_ge(s["w_hi_dve"], n + 1)
                dve.tensor_tensor(w_att[:, n, 1, :, :], w_att_raw[:, n, 1, :, :], w_att[:, n, 0, :, :].bitcast(fp32),
                                  ALU.subtract).then_inc(s["w_lo_dve"], 1)

            def maximum(it, g, heads):
                G = it * NG + g + 2
                if not group(G):
                    return
                for h in heads:
                    n = G * 4 + h
                    wait(dve, "max_mm", n + 1)
                    dve.tensor_reduce(out=negm[:, :, h:h + 1], in_=psum[:, MX + h % 2, :].rearrange("p (t k) -> p t k", t=TT),
                                      axis=AX.X, op=ALU.max, negate=True).then_inc(s["max_taken"], 1)
                if heads[-1] == GH - 1:
                    wait(dve, "max_taken", (G + 1) * 4)
                    wait(dve, "m_tr", G)
                    dve.tensor_copy(m12[:, :, GH:2 * GH], negm[:, :, :]).then_inc(s["m_hi_done"], 1)
                    wait(dve, "m_hi_done", G + 1)
                    dve.tensor_tensor(m12[:, :, 2 * GH:3 * GH], negm[:, :, :], m12[:, :, GH:2 * GH].bitcast(fp32),
                                      ALU.subtract).then_inc(s["m_lo_done"], 1)

            def statistics(b, tiles, stats_sem, mv_sem, var_sem):
                n = len(tiles)
                for t, j in enumerate(tiles):
                    dve.bn_stats(stats[:, t, :], hidden_tile(j)).then_inc(s[stats_sem], 1)
                wait(dve, stats_sem, (b + 1) * n)
                dve.memset(scratch[:, :], 0.0)
                for t in range(n):
                    dve.bn_aggr(mv[:, t, :], stats[:, t, :]).then_inc(s[mv_sem], 1)
                wait(dve, mv_sem, (b + 1) * n)
                dve.tensor_scalar_add(vareps[:, 0:n], mv[:, 0:n, 1], EPS).then_inc(s[var_sem], 1)

            def add_hidden(it, t):
                b = it - 1
                wait(dve, "c_proj", b * 2 + (t + 1))
                wait(dve, "cb_added", (b + 1) * 2)
                h = hidden_tile(b * TT + t)
                dve.tensor_tensor(h, in_bank("c", t), h, ALU.add).then_inc(s["hidden_added"], 1)

            def add_values(it, t):
                b = it + 1
                wait(dve, "v_proj", b * 2 + (t + 1))
                wait(dve, "v_split", b)
                dve.tensor_tensor(v32[:, t, :], in_bank("v", t), vb_bc[:, :], ALU.add).then_inc(s["v_added"], 1)

            def step(it, g):
                maximum(it, g, (0, 1))
                if g == 1 and batch(it):
                    wait(dve, "v_cast", it * 2 + 1)
                    v = v32[:, :, :].rearrange("p c (h d) -> p c h d", h=H)
                    for kc in range(KC):
                        ins = dve.tensor_tensor(v[:, kc], v[:, kc], vparts[:, kc, :, 1:1 + HD], ALU.subtract)
                    ins.then_inc(s["v_rest"], 1)
                G = it * NG + g + 3
                if group(G):
                    wait(dve, "qk_hi_done", (G + 1) * 2)
                    for n, col in ((0, QB), (1, KB_)):
                        piece = slice(n * LQ, (n + 1) * LQ)
                        dve.scalar_tensor_tensor(out=qk[:, 3 * n, :], in0=in_bank("qk", g)[:, piece],
                                                 scalar=cols[:, col + (g + 3) % NG:col + (g + 3) % NG + 1],
                                                 in1=qk[:, 1 + n, :].bitcast(fp32), op0=ALU.add,
                                                 op1=ALU.subtract).then_inc(s["qk_lo_done"], 1)
                if g == 1 and batch(it):
                    wait(dve, "v_cast", it * 2 + 2)
                    for kc in range(KC):
                        ins = dve.tensor_tensor(vparts[:, kc, :, 1 + 2 * HD:VW], v[:, kc],
                                                vparts[:, kc, :, 1 + HD:1 + 2 * HD], ALU.subtract)
                    ins.then_inc(s["v_split"], 1)
                maximum(it, g, (2, 3))
                if g == 0 and batch(it + 1):
                    b = it + 1
                    wait(dve, "x_affine", (b + 1) * 4)
                    wait(dve, "ctx_copied", (b + 1) * 2)
                    wait(dve, "qk_proj", b * NG)
                    wait(dve, "v_proj", b * 2)
                    for n, dst in ((0, xs), (1, cs)):
                        dve.tensor_copy(dst[:, 0, :, :], xc_t[:, n, :, :]).then_inc(s["split_hi"], 1)
                    for n, dst in ((0, xs), (1, cs)):
                        wait(dve, "split_hi", b * 2 + (n + 1))
                        dve.tensor_tensor(dst[:, 1, :, :], xc_t[:, n, :, :], dst[:, 0, :, :].bitcast(fp32),
                                          ALU.subtract).then_inc(s["split_lo"], 1)
                if g == 1:
                    if batch(it + 1):
                        add_values(it, 0)
                    if batch(it - 1):
                        b = it - 1
                        for j in range(2):
                            wait(dve, "att_hi_done", b * 2 + (j + 1))
                            dve.tensor_tensor(att_t[:, 1, 2 * j:2 * j + 2, :], in_bank("att", j).rearrange("p (k q) -> p k q", k=2),
                                              att_t[:, 0, 2 * j:2 * j + 2, :].bitcast(fp32), ALU.subtract).then_inc(s["att_lo_done"], 1)
                    if batch(it + 2):
                        b = it + 2
                        wait(dve, "x_loaded", (b + 1) * 16)
                        wait(dve, "ln_rstd", b)
                        wait(dve, "x_normed", b * 2)
                        statistics(b, [b * TT + t for t in range(TT)], "ln_stats", "ln_mv", "ln_var")
                if g == 2:
                    if batch(it + 1):
                        add_values(it, 1)
                    if batch(it - 1):
                        add_hidden(it, 0)
                    if batch(it + 2):
                        b = it + 2
                        wait(dve, "ln_rstd", b + 1)
                        wait(dve, "x_tr", b * 2)
                        for t in range(TT):
                            dve.tensor_scalar(xn[:, t, :], hidden_tile(b * TT + t), mv[:, t, 0:1], rstd[:, t:t + 1],
                                              ALU.subtract, ALU.mult).then_inc(s["x_normed"], 1)
                if g == 3 and batch(it - 1):
                    add_hidden(it, 1)
                G = it * NG + g - 1
                if group(G):
                    if (g - 1) % NG == 0:
                        wait(dve, "att_tr", it * 2)
                    for t in range(TT):
                        wait(dve, "pv_mm", G * 2 + (t + 1))
                        rows = psum[:, PV + t, 0:GH * VW].rearrange("p (h c) -> p h c", c=VW)
                        h0 = GH * ((g - 1) % NG)
                        dve.tensor_reduce(out=att[:, t, h0 * HD:(h0 + GH) * HD].rearrange("p (h d) -> p h d", h=GH),
                                          in_=rows[:, :, 1:VW].rearrange("p h (s d) -> p h d s", s=3),
                                          axis=AX.X, op=ALU.add).then_inc(s["pv_taken"], 1)
                        dve.reciprocal(rl[:, t, h0:h0 + GH], rows[:, :, 0]).then_inc(s["pv_taken"], 1)

            iterations(dve, step)

            def weights(i):
                dve.wait_ge(w2_loaded[i], 32)
                dve.tensor_copy(w_mlp[i][:, 0::2, :], w_mlp_raw[i][:, 1::2, :]).then_inc(s["w2_hi"], 1)
                dve.wait_ge(s["w2_hi"], i + 1)
                dve.tensor_tensor(w_mlp[i][:, 1::2, :], w_mlp_raw[i][:, 1::2, :], w_mlp[i][:, 0::2, :].bitcast(fp32),
                                  ALU.subtract).then_inc(s["w2_lo"], 1)

            def ln2_stats(j):
                wait(dve, "y_rstd", j)
                wait(dve, "y_normed", j)
                statistics(j, [j], "y_stats", "y_mv", "y_var")

            def ln2_norm(j, t):
                wait(dve, "y_rstd", j + 1)
                wait(dve, "y_tr", j - 1)
                dve.tensor_scalar(yn[:, t % 2, :], hidden_tile(j), mv[:, 0, 0:1], rstd[:, 0:1],
                                  ALU.subtract, ALU.mult).then_inc(s["y_normed"], 1)

            def split_y(c):
                wait(dve, "y_affine", (c + 1) * CH * KT)
                wait(dve, "fc_mm", c * FT)
                for k in range(KT):
                    dve.tensor_copy(y_hi[:, k, :], y_t[:, k, :]).then_inc(s["y_hi_done"], 1)
                    wait(dve, "y_hi_done", c * KT + (k + 1))
                    dve.tensor_tensor(y_lo[:, k, :], y_t[:, k, :], y_hi[:, k, :].bitcast(fp32),
                                      ALU.subtract).then_inc(s["y_lo_done"], 1)

            def split_h(F, f):
                wait(dve, "h_done", F + 1)
                wait(dve, "proj_mm", F - 1)
                dve.tensor_copy(h_hi[:, f % 2, :], h32[:, f % 2, :]).then_inc(s["h_hi_done"], 1)
                wait(dve, "h_hi_done", F + 1)
                dve.tensor_tensor(h_lo[:, f % 2, :], h32[:, f % 2, :], h_hi[:, f % 2, :].bitcast(fp32),
                                  ALU.subtract).then_inc(s["h_lo_done"], 1)

            def add_out(c):
                wait(dve, "proj_mm", (c + 1) * FT)
                for t in range(CH):
                    wait(dve, "pb_added", c * CH + (t + 1))
                    h = hidden_tile(c * CH + t)
                    dve.tensor_tensor(h, psum[:, ACC + t, :], h, ALU.add).then_inc(s["out_added"], 1)

            wait(dve, "c_proj", B * 2)
            wait(dve, "hidden_added", B * 2)
            for t in range(CH):
                ln2_stats(t)
                if t == 0:
                    weights(0)
                ln2_norm(t, t)
            split_y(0)
            weights(1)
            split_h(0, 0)

            def body(c, first):
                for i in range(FT):
                    if i == 0 and not first:
                        add_out(c - 1)
                    if first and i + 2 < FT:
                        weights(i + 2)
                    if i < FT - 1:
                        split_h(c * FT + (i + 1), i + 1)
                    elif has_next(c):
                        split_y(c + 1)
                        split_h(c * FT + FT, 0)
                    if has_next(c):
                        for t in range(CH):
                            if i == 3 * t + 1:
                                ln2_stats(c * CH + (CH + t))
                            if i == 3 * t + 2:
                                ln2_norm(c * CH + (CH + t), t)

            chunks(dve, body)
            add_out(CHUNKS - 1)

        @block.tensor
        def _(pe):
            def three_passes(out_ap, pairs, last_sem=None):
                n = len(pairs)
                for i, (a_hi, a_lo, b_hi, b_lo) in enumerate(pairs):
                    nc.tensor.matmul(out_ap, a_hi, b_hi, start=(i == 0), stop=False)
                    nc.tensor.matmul(out_ap, a_hi, b_lo, start=False, stop=False)
                    ins = nc.tensor.matmul(out_ap, a_lo, b_hi, start=False, stop=(i == n - 1))
                return ins

            pe.wait_ge(s["ident_ready"], 1)

            def transposed_scores(it, g, pair):
                G = it * NG + g
                if not group(G):
                    return
                if pair == 0:
                    wait(pe, "m_stored", (G + 1) * 48)
                for kc in range(KC):
                    n = G * 4 + 2 * pair + kc
                    wait(pe, "p_hi_done", n - 1)
                    for hh in range(2):
                        h = GH * g + 2 * pair + hh
                        ins = nc.tensor.matmul(psum[:, ST + kc, hh * LQ:(hh + 1) * LQ],
                                               kst[0:SUBROWS, h, kc * P:(kc + 1) * P], qst[0:SUBROWS, h, :],
                                               start=True, stop=True)
                    ins.then_inc(s["st_mm"], 1)

            def scores(it, g, heads):
                G = it * NG + g + 2
                if not group(G):
                    return
                if heads[0] == 0:
                    wait(pe, stack_filled[g % 2], fills_upto(G, g % 2))
                    wait(pe, "pool_consts", 5)
                for hh in heads:
                    h = GH * ((g + 2) % NG) + hh
                    wait(pe, "max_taken", G * 4 + (hh - 1))
                    for t in range(TT):
                        ins = nc.tensor.matmul(psum[:, MX + hh % 2, t * LK:(t + 1) * LK],
                                               qst[0:MAXROWS, h, t * P:(t + 1) * P], kst[0:MAXROWS, h, :],
                                               start=True, stop=True)
                    ins.then_inc(s["max_mm"], 1)

            def project_qk(it, g):
                G = it * NG + g + 3
                if not group(G):
                    return
                b = it if g == 0 else it + 1
                wait(pe, "split_lo", (b + 1) * 2)
                wait(pe, "w_lo_dve", 2)
                bank = bank_of(it, "qk", g)
                c0 = P * ((g + 3) % NG)
                for n, src in ((0, xs), (1, cs)):
                    ins = three_passes(bank[:, n * LQ:(n + 1) * LQ],
                                       [(w_att[:, n, 0, k, c0:c0 + P], w_att[:, n, 1, k, c0:c0 + P],
                                         src[:, 0, k, :], src[:, 1, k, :]) for k in range(KT)])
                ins.then_inc(s["qk_proj"], 1)

            def project_v(it, t):
                if not batch(it + 1):
                    return
                wait(pe, "w_lo_pool", 1)
                bank = bank_of(it, "v", t)
                three_passes(bank, [(cs[:, 0, k, t * P:(t + 1) * P], cs[:, 1, k, t * P:(t + 1) * P],
                                     w_att[:, 2, 0, k, :], w_att[:, 2, 1, k, :]) for k in range(KT)]).then_inc(s["v_proj"], 1)

            def project_c(it, t):
                if not batch(it - 1):
                    return
                wait(pe, "att_lo_done", it * 2)
                wait(pe, "w_lo_pool", 2)
                bank = bank_of(it, "c", t)
                three_passes(bank, [(att_t[:, 0, k, t * P:(t + 1) * P], att_t[:, 1, k, t * P:(t + 1) * P],
                                     w_att[:, 3, 0, k, :], w_att[:, 3, 1, k, :]) for k in range(KT)]).then_inc(s["c_proj"], 1)

            def transposes(it, kind, b, src, ready, per_batch, done):
                if not batch(b):
                    return
                wait(pe, ready, (b + 1) * per_batch)
                for j in range(2):
                    bank = bank_of(it, kind, j)
                    for i in range(2):
                        for t in range(TT):
                            k = 2 * j + i
                            ins = nc.tensor.transpose(bank[:, i * LQ + t * P:i * LQ + (t + 1) * P],
                                                      src[:, t, k * P:(k + 1) * P], ident[:, :])
                    ins.then_inc(s[done], 1)

            def values(it, g):
                G = it * NG + g - 1
                if not group(G):
                    return
                b = it - 1 if g == 0 else it
                wait(pe, "p_lo_done", (G + 1) * 4)
                wait(pe, "v_split", b + 1)
                gp = (g - 1) % NG
                for t in range(TT):
                    wait(pe, "pv_taken", (G - 1) * 4 + (2 * t + 2))
                    for hh in range(GH):
                        o = psum[:, PV + t, hh * VW:(hh + 1) * VW]
                        for kc in range(KC):
                            slot = (gp % 2) * 4 + (hh // 2) * 2 + kc
                            cut = slice((hh % 2) * LQ + t * P, (hh % 2) * LQ + (t + 1) * P)
                            nc.tensor.matmul(o, p_hi[:, slot, cut], vparts[:, kc, GH * gp + hh, :],
                                             start=(kc == 0), stop=False)
                            ins = nc.tensor.matmul(o[:, 0:VW_LO], p_lo[:, slot, cut], vparts[:, kc, GH * gp + hh, 0:VW_LO],
                                                   start=False, stop=(kc == KC - 1))
                    ins.then_inc(s["pv_mm"], 1)

            def transpose_max(it, g):
                G = it * NG + g + 2
                if not group(G):
                    return
                wait(pe, "m_lo_done", G + 1)
                bank = bank_of(it, "m", g)
                for t in range(TT):
                    ins = nc.tensor.transpose(bank[0:3 * GH, t * P:(t + 1) * P], m12[:, t, :].bitcast(fp32), ident[:, :])
                ins.then_inc(s["m_tr"], 1)

            def step(it, g):
                transposed_scores(it, g, 0)
                scores(it, g, (0, 1))
                project_qk(it, g)
                transposed_scores(it, g, 1)
                scores(it, g, (2, 3))
                if g == 1:
                    project_v(it, 0)
                    transposes(it, "att", it - 1, att, "att_normed", 2, "att_tr")
                if g == 2:
                    project_v(it, 1)
                    project_c(it, 0)
                if g == 3:
                    project_c(it, 1)
                    transposes(it, "x", it + 2, xn, "x_normed", 2, "x_tr")
                    transposes(it, "ctx", it + 2, ctx_sb, "ctx_loaded", 16, "ctx_tr")
                values(it, g)
                transpose_max(it, g)

            iterations(pe, step)

            def fc(c, F, f):
                wait(pe, "w2_lo", f + 1)
                wait(pe, "h_done", F - 1)
                for k in range(KT):
                    wait(pe, "y_lo_done", c * KT + (k + 1))
                    w = w_mlp[f][:, :, k * P:(k + 1) * P]
                    ins = None
                    bank = psum[:, FC + f % 2, :]
                    nc.tensor.matmul(bank, w[:, 0, :], y_hi[:, k, :], start=(k == 0), stop=False)
                    nc.tensor.matmul(bank, w[:, 0, :], y_lo[:, k, :], start=False, stop=False)
                    ins = nc.tensor.matmul(bank, w[:, 1, :], y_hi[:, k, :], start=False, stop=(k == KT - 1))
                ins.then_inc(s["fc_mm"], 1)

            def proj(c, F, f):
                wait(pe, "h_lo_done", F + 1)
                for t in range(CH):
                    if f == 0:
                        wait(pe, "out_added", (c - 1) * CH + (t + 1))
                    cut = slice(t * P, (t + 1) * P)
                    acc = psum[:, ACC + t, :]
                    nc.tensor.matmul(acc, h_hi[:, f % 2, cut], w_mlp[f][:, 2, :], start=(f == 0), stop=False)
                    nc.tensor.matmul(acc, h_hi[:, f % 2, cut], w_mlp[f][:, 3, :], start=False, stop=False)
                    ins = nc.tensor.matmul(acc, h_lo[:, f % 2, cut], w_mlp[f][:, 2, :], start=False, stop=(f == FT - 1))
                ins.then_inc(s["proj_mm"], 1)

            def transpose_y(j, t):
                wait(pe, "y_normed", j + 1)
                wait(pe, "y_affine", (j - 1) * KT)
                for k in range(KT):
                    ins = nc.tensor.transpose(psum[:, TR + t % 2, k * P:(k + 1) * P], yn[:, t % 2, k * P:(k + 1) * P], ident[:, :])
                ins.then_inc(s["y_tr"], 1)

            for t in range(CH):
                transpose_y(t, t)
            fc(0, 0, 0)

            def body(c, first):
                for i in range(FT):
                    if i < FT - 1:
                        fc(c, c * FT + (i + 1), i + 1)
                    elif has_next(c):
                        fc(c + 1, c * FT + FT, 0)
                    if has_next(c) and i % 3 == 0 and 3 <= i <= 12:
                        t = i // 3 - 1
                        transpose_y(c * CH + (CH + t), t)
                    proj(c, c * FT + i, i)

            chunks(pe, body)


def mybir_f32(v):
    import numpy as np
    return np.float32(v)


_INS = ["x", "ctx_2048", "mask_BxS2_bf1"] + ["L0_xattn_" + n for n in (
    "ln1_w", "ln1_b", "q_w", "q_b", "k_w", "k_b", "v_w", "v_b", "cproj_w", "cproj_b",
    "ln2_w", "ln2_b", "fc_w", "fc_b", "proj_w", "proj_b")]
_OUTS = [((8, 256, 512), "float32")]


def kernel(**inputs):
    import numpy as _np
    import concourse.bacc as _bacc
    from concourse import mybir as _mybir
    from concourse.bass_utils import run_bass_kernel_spmd as _run

    nc = _bacc.Bacc("TRN2", target_bir_lowering=False, num_devices=1)
    arrays, args = {}, []
    for name in _INS:
        a = _np.ascontiguousarray(inputs[name])
        if a.dtype == _np.bool_:
            a = a.view(_np.uint8)
        arrays[f"in_{name}_dram"] = a
        args.append(nc.dram_tensor(f"in_{name}_dram", a.shape, _mybir.dt.from_np(a.dtype), kind="ExternalInput").ap())
    for i, (shape, dtype) in enumerate(_OUTS):
        dt = _mybir.dt.from_np(_np.dtype(dtype))
        args.append(nc.dram_tensor(f"out_{i}_dram", shape, dt, kind="ExternalOutput").ap())
    xattn_kernel(nc, *args)
    r = _run(nc, [arrays], core_ids=[0])
    got = tuple(r.results[0][f"out_{i}_dram"] for i in range(len(_OUTS)))
    return got[0]
```

```python
import concourse.bass as bass
from concourse import mybir
from contextlib import ExitStack

fp32 = mybir.dt.float32
fp32r = mybir.dt.float32r
bf16 = mybir.dt.bfloat16
fp16 = mybir.dt.float16
u8 = mybir.dt.uint8
ALU = mybir.AluOpType
ACT = mybir.ActivationFunctionType
AX = mybir.AxisListType


def xattn_kernel(nc, x, ctx_in, mask, ln1_w, ln1_b, q_w, q_b, k_w, k_b, v_w, v_b, c_w, c_b,
                 ln2_w, ln2_b, fc_w, fc_b, proj_w, proj_b, out):
    B, LQ, D = x.shape
    LK = ctx_in.shape[1]
    H, HD = 16, 32
    INNER = fc_w.shape[1]
    P = 128
    KT = D // P
    TT = LQ // P
    KC = LK // P
    GH = P // HD
    NG = H // GH
    GROUPS = B * NG
    FT = INNER // P
    CH = 4
    CW = CH * P
    CHUNKS = B * LQ // CW
    VW = 1 + 3 * HD
    VW_LO = 1 + 2 * HD
    SCALE = float(HD) ** -0.5
    EPS = 1e-5
    PSHIFT = 7.5
    MASKED = float(2.0 ** 127)
    MAXROWS = 3 * HD + 1
    SUBROWS = 3 * HD + 3
    SCALE32 = float(mybir_f32(SCALE))

    ctx = ExitStack()
    with ctx:
        def sb(name, shape, dt, offset):
            return nc.alloc_sbuf_tensor_at(name, shape, dt, offset=offset)

        BASE = 16512
        KB = 1024
        hidden = sb("hidden", [P, B * TT, D], fp32, BASE)
        C0 = BASE + 32 * KB
        ident = sb("ident", [P, P], fp32, C0)
        cols = sb("cols", [P, 6 * KT + FT], fp32, C0 + 512)
        maskcol = sb("maskcol", [P, B * KC], fp32, C0 + 704)
        maskcol_raw = sb("maskcol_raw", [P, B * KC], u8, C0 + 768)
        stats = sb("stats", [P, 2, 6], fp32, C0 + 800)
        mv = sb("mv", [P, 2, 2], fp32, C0 + 864)
        rstd = sb("rstd", [P, 2], fp32, C0 + 896)
        mhalf = sb("mhalf", [P, 2], fp32, C0 + 928)
        vareps = sb("vareps", [P, 2], fp32, C0 + 960)
        maskbias = sb("maskbias", [P, KC], fp32, C0 + 992)
        scratch = sb("scratch", [P, 1], fp32, C0 + 1024)
        R0 = C0 + 1056

        w_att = sb("w_att", [P, 4, 2, KT, D], fp32r, R0)
        w_att_raw = sb("w_att_raw", [P, 4, 2, KT, D], fp32, R0)
        A1 = R0 + 64 * KB
        stacks = sb("stacks", [P, H, 2, LQ], fp32r, A1)
        qst, kst = stacks[:, :, 0], stacks[:, :, 1]
        A2 = A1 + 32 * KB
        att_t = sb("att_t", [P, 2, KT, LQ], fp32r, A2)
        p32 = sb("p32", [P, 2, 2 * LQ], fp32, A2 + 8 * KB)
        p_hi = sb("p_hi", [P, 8, 2 * LQ], fp16, A2 + 12 * KB)
        p_lo = sb("p_lo", [P, 8, 2 * LQ], fp16, A2 + 20 * KB)
        vparts = sb("vparts", [P, KC, H, VW], bf16, A2 + 28 * KB)
        A3 = R0 + 131 * KB
        xs = sb("xs", [P, 2, KT, LQ], fp32r, A3)
        cs = sb("cs", [P, 2, KT, LK], fp32r, A3 + 8 * KB)
        ctx_sb = sb("ctx_sb", [P, KC, D], fp32, A3 + 16 * KB)
        xn = sb("xn", [P, TT, D], fp32, A3 + 20 * KB)
        x_t = sb("x_t", [P, KT, LQ], fp32, A3 + 20 * KB)
        qk = sb("qk", [P, 4, LQ], fp32r, A3 + 24 * KB)
        v32 = sb("v32", [P, KC, D], fp32, A3 + 28 * KB)
        A4 = A3 + 32 * KB
        att = sb("att", [P, TT, D], fp32, A4)
        vb_bc = sb("vb_bc", [P, D], fp32, A4 + 4 * KB)
        cb_bc = sb("cb_bc", [P, D], fp32, A4 + 6 * KB)
        A5 = A4 + 8 * KB
        negm = sb("negm", [P, TT, GH], fp32, A5)
        m12 = sb("m12", [P, TT, 3 * GH], fp32r, A5 + 32)
        rl = sb("rl", [P, TT, H], fp32, A5 + 160)
        mrow = sb("mrow", [3 * GH, LQ], fp32r, A5 + 288)
        mrow_raw = sb("maskrow_raw", [B, LK], u8, A5 + 288 + KB)
        maskrow = sb("maskrow", [B, 2, LK], fp32, A5 + 544 + KB)
        w_mlp = [sb(f"w_mlp{i}", [P, 4, D], fp32r, R0 + 8 * KB * i) for i in range(FT)]
        w_mlp_raw = [sb(f"w_mlp_raw{i}", [P, 4, D], fp32, R0 + 8 * KB * i) for i in range(FT)]
        y_hi = sb("y_hi", [P, KT, CW], fp32r, A3)
        y_lo = sb("y_lo", [P, KT, CW], fp32r, A3 + 8 * KB)
        yn = sb("yn", [P, 2, D], fp32, A3 + 16 * KB)
        y_t = sb("y_t", [P, KT, CW], fp32, A3 + 20 * KB)
        h32 = sb("h32", [P, 2, CW], fp32, A3 + 28 * KB)
        h_hi = sb("h_hi", [P, 2, CW], fp32r, A3 + 32 * KB)
        h_lo = sb("h_lo", [P, 2, CW], fp32r, A3 + 36 * KB)
        pb_bc = sb("pb_bc", [P, D], fp32, A3 + 40 * KB)
        assert A3 + 42 * KB <= 229344 and A5 + 544 + 3 * KB <= 229344

        mask_rows = nc.dram_tensor("mask_rows", [B, 2, LK], fp32, kind="Internal").ap()
        qk_rows = nc.dram_tensor("qk_rows", [2, HD, GH, 4, LQ], fp32, kind="Internal").ap()

        LN1W, LN1B, QB, KB_, LN2W, LN2B, FCB = [KT * i for i in range(7)]

        psum = ctx.enter_context(nc.psum_tensor("psum", [P, 8, 512], fp32))
        ST, MX, PV, MS = 0, 2, 4, 6
        ACC, FC, TR = (0, 1, 6, 7), 2, 4

        def turned(c, t):
            return psum[:, (FC if isinstance(c, int) and c == 0 else TR) + t % 2, :]

        names = """x_loaded ctx_loaded ln1_loaded qkb_loaded small_loaded mlp_columns_loaded mask_stored out_stored
            ident_zero ident_ready pool_consts zeros_ready mask_ready maskbias_ready
            wq_loaded wk_loaded wv_loaded wc_loaded w_hi_qk w_hi_act w_lo_dve w_lo_pool
            qk_proj x_tr ctx_tr max_mm st_mm pv_mm m_tr att_tr v_proj c_proj
            x_affine qk_hi_done qk_lo_done p_hi_done p_lo_done mrow_ready att_hi_done att_lo_done
            v_cast v_rest v_split v_added max_taken m_hi_done m_lo_done pv_taken att_normed hidden_added
            ln_stats ln_mv ln_var ln_rstd x_normed cb_added x_hi_done x_lo_done ctx_hi_done ctx_lo_done
            qk_stored stack_filled0 stack_filled1 m_stored
            w2_hi w2_lo fc_mm proj_mm y_tr y_affine y_normed y_hi_done y_lo_done h_done h_hi_done h_lo_done
            pb_loaded pb_added out_added y_stats y_mv y_var y_rstd""".split()
        s = {n: ctx.enter_context(nc.semaphore(n)) for n in names}
        w2_loaded = [ctx.enter_context(nc.semaphore(f"w2_loaded{i}")) for i in range(FT)]
        stack_filled = [s["stack_filled0"], s["stack_filled1"]]
        SMALL = 4 * 16
        FILLS = (3 + 1) * 16

        def wait(eng, sem, value):
            if not isinstance(value, int) or value > 0:
                eng.wait_ge(s[sem] if isinstance(sem, str) else sem, value)

        def batch(b):
            return not isinstance(b, int) or 0 <= b < B

        def group(G):
            return not isinstance(G, int) or 0 <= G < GROUPS

        USES = [("qk", 0), ("ctx", 0), ("ctx", 1), ("m", 0), ("c", 1),
                ("qk", 1), ("m", 1), ("att", 0), ("att", 1), ("v", 0),
                ("qk", 2), ("m", 2), ("v", 1),
                ("qk", 3), ("m", 3), ("c", 0), ("x", 0), ("x", 1)]

        def emptied(it, kind, n):
            if kind in ("qk", "m"):
                G = it * NG + n + (3 if kind == "qk" else 1)
                if not group(G):
                    return None
                return ("qk_lo_done", (G + 1) * 2) if kind == "qk" else ("mrow_ready", G + 1)
            b = it + {"v": 1, "att": -1, "c": -1 - n, "x": 2, "ctx": 1}[kind]
            if not batch(b):
                return None
            return {"v": ("v_added", b * 2 + (n + 1)), "att": ("att_lo_done", b * 2 + (n + 1)),
                    "c": ("hidden_added", b * 2 + (n + 1)), "x": ("x_affine", b * 4 + 2 * (n + 1)),
                    "ctx": ("ctx_lo_done", b * 2 + (n + 1))}[kind]

        def bank_of(it, kind, n):
            k = USES.index((kind, n))
            for back in range(k - 2, k - 2 - 2 * len(USES), -2):
                before = emptied(it + back // len(USES), *USES[back % len(USES)])
                if before:
                    wait(nc.tensor, *before)
                    break
            return psum[:, MS + k % 2, :]

        def in_bank(kind, n):
            return psum[:, MS + USES.index((kind, n)) % 2, :]

        def iterations(eng, step, weights=None, tail=None):
            for g in range(2, NG):
                step(-2, g)
            step(-1, 0)
            if weights:
                weights()
            for g in range(1, NG):
                step(-1, g)
            for it in (0, 1):
                for g in range(NG):
                    step(it, g)
            with eng.Fori(2, B - 2) as it:
                for g in range(NG):
                    step(it, g)
            for it in (B - 2, B - 1, B):
                for g in range(NG):
                    step(it, g)
                    if tail and it >= B - 1:
                        tail(it, g)
            step(B + 1, 0)

        def chunks(eng, body):
            body(0, True)
            with eng.Fori(1, CHUNKS - 1) as c:
                body(c, False)
            body(CHUNKS - 1, False)

        def has_next(c):
            return not isinstance(c, int) or c < CHUNKS - 1

        def hidden_tile(j):
            if isinstance(j, int):
                return hidden[:, j, :]
            return hidden[:, bass.ds(j, 1), :].rearrange("p o d -> p (o d)")

        def fills_upto(G, parity):
            if isinstance(G, int):
                return (G // 2 + 1) * FILLS if G >= 0 else 0
            return (G - parity) * (FILLS // 2) + FILLS

        block = ctx.enter_context(nc.Block())

        @block.sync
        def _(sp):
            def address_follows():
                sp.wait_ge(s["pool_consts"], 1)

            def load_x(b):
                if not isinstance(b, int) or b > 0:
                    wait(sp, "x_loaded", b * 16)
                    address_follows()
                sp.dma_start(hidden[:, bass.ds(b * TT, TT), :] if not isinstance(b, int) else hidden[:, b * TT:(b + 1) * TT, :],
                             x_rows(x, b)).then_inc(s["x_loaded"], 16)

            def load_ctx(b):
                if not isinstance(b, int) or b > 0:
                    wait(sp, "ctx_tr", b * 2)
                    address_follows()
                sp.dma_start(ctx_sb[:, :, :], x_rows(ctx_in, b)).then_inc(s["ctx_loaded"], 16)

            def x_rows(src, b):
                rows = src[b:b + 1] if isinstance(b, int) else src[bass.ds(b, 1)]
                return rows.rearrange("o (t p) d -> p (o t) d", p=P)

            load_x(0)
            load_ctx(0)
            for n, (w, sem) in enumerate(((q_w, "wq_loaded"), (k_w, "wk_loaded"), (v_w, "wv_loaded"), (c_w, "wc_loaded"))):
                sp.dma_start(w_att_raw[:, n, 1, :, :], w.rearrange("(k p) n -> p k n", p=P)).then_inc(s[sem], 16)
            load_x(1)
            sp.wait_ge(s["mask_ready"], 2)
            sp.wait_ge(s["pool_consts"], 5)
            sp.dma_start(mask_rows, maskrow[:, :, :]).then_inc(s["mask_stored"], 16)
            sp.wait_ge(s["mask_stored"], 16)

            def step(it, g):
                G = it * NG + g + 3
                b = it if g == 0 else it + 1
                if g == 0 and batch(it + 2) and not (isinstance(it, int) and it == -1):
                    load_x(it + 2)
                if g == 1 and batch(it + 2):
                    load_ctx(it + 2)
                if group(G):
                    scratch_rows = qk_rows[(g + 3) % 2]
                    filled = stack_filled[(g + 3) % 2]
                    wait(sp, filled, fills_upto(G - 2, (g + 3) % 2))
                    address_follows()
                    wait(sp, "qk_lo_done", (G + 1) * 2)
                    sp.dma_start(scratch_rows.rearrange("d h n q -> h d n q"), qk[:, :, :].bitcast(fp32)).then_inc(s["qk_stored"], 16)
                if group(G - 2):
                    slot = slice(GH * ((g + 1) % NG), GH * ((g + 1) % NG) + GH)
                    address_follows()
                    wait(sp, "mrow_ready", G - 1)
                    sp.dma_start(qst[3 * HD:3 * HD + 3, slot, :].bitcast(fp32),
                                 mrow[:, :].bitcast(fp32)).then_inc(s["m_stored"], 16)
                if group(G):
                    slot = slice(GH * ((g + 3) % NG), GH * ((g + 3) % NG) + GH)
                    row = mask_rows[b:b + 1] if isinstance(b, int) else mask_rows[bass.ds(b, 1)]
                    sp.dma_start(stacks[3 * HD:3 * HD + 1, slot, :, :].bitcast(fp32),
                                 row.rearrange("b (o n) q -> b o n q", o=1).to_broadcast([1, GH, 2, LK])).then_inc(filled, 16)
                    address_follows()
                    wait(sp, "qk_stored", (G + 1) * 16)
                    for r, parts in enumerate((slice(1, 3), slice(1, 4, 2), slice(0, 3, 2))):
                        sp.dma_start(stacks[HD * r:HD * r + HD, slot, :, :].bitcast(fp32),
                                     scratch_rows[:, :, parts, :]).then_inc(filled, 16)
            def load_tile(i):
                sp.dma_start(w_mlp_raw[i][:, 1, :].rearrange("p (k f) -> p k f", k=KT),
                             fc_w[:, i * P:(i + 1) * P].rearrange("(k p) f -> p k f", p=P)).then_inc(w2_loaded[i], 16)
                sp.dma_start(w_mlp_raw[i][:, 3, :], proj_w[i * P:(i + 1) * P, :]).then_inc(w2_loaded[i], 16)

            def tail(it, g):
                if it == B - 1 and g == 0:
                    wait(sp, "qk_proj", GROUPS)
                    wait(sp, "v_proj", B * 2)
                if it == B - 1 and g < 3:
                    load_tile(2 * g)
                    load_tile(2 * g + 1)

            iterations(sp, step, tail=tail)

            wait(sp, "c_proj", B * 2)
            sp.dma_start(pb_bc[:, :], proj_b.rearrange("(o n) -> o n", o=1).to_broadcast([P, D])).then_inc(s["pb_loaded"], 16)
            for i in range(6, FT):
                load_tile(i)

            def store(c, first):
                for t in range(CH):
                    wait(sp, "out_added", c * CH + (t + 1))
                    address_follows()
                    rows = out_rows(c * CH + t)
                    src = hidden[:, c * CH + t, :] if isinstance(c, int) else hidden[:, bass.ds(c * CH + t, 1), :].rearrange("p o d -> p (o d)")
                    sp.dma_start(rows, src).then_inc(s["out_stored"], 16)

            def out_rows(j):
                flat = out.rearrange("b (t p) d -> (b t) p d", p=P)
                return flat[j] if isinstance(j, int) else flat[bass.ds(j, 1)].rearrange("o p d -> (o p) d")

            chunks(sp, store)
            sp.wait_ge(s["out_stored"], 16 * B * TT)

        @block.gpsimd
        def _(pool):
            def small(dst, src, sem):
                with nc.allow_non_contiguous_dma(reason="per-partition vectors, a few KB"):
                    pool.dma_start(dst, src).then_inc(s[sem], 16)

            def column(v):
                return v.rearrange("(k p) -> p k", p=P)

            def repeated(v):
                return v.rearrange("(o n) -> o n", o=1).to_broadcast([P, D])

            small(cols[:, LN1W:LN1W + KT], column(ln1_w), "ln1_loaded")
            small(cols[:, LN1B:LN1B + KT], column(ln1_b), "ln1_loaded")
            pool.memset(ident[:, :], 0.0).then_inc(s["ident_zero"], 1)
            pool.wait_ge(s["ident_zero"], 1)
            pool.affine_select(out=ident[:, :], in_=ident[:, :], compare_op=ALU.not_equal, fill=1.0,
                               base=0, pattern=[[-1, P]], channel_multiplier=1).then_inc(s["ident_ready"], 1)
            pool.memset(mhalf[:, :], -0.5).then_inc(s["pool_consts"], 1)
            small(cols[:, QB:QB + KT], column(q_b), "qkb_loaded")
            small(cols[:, KB_:KB_ + KT], column(k_b), "qkb_loaded")
            small(mrow_raw[:, :], mask, "small_loaded")
            pool.wait_ge(s["pool_consts"], 1)

            def inverse_std(b, n, var_sem, out_sem):
                wait(pool, var_sem, b + 1)
                pool.tensor_tensor(rstd[:, 0:n], vareps[:, 0:n], mhalf[:, 0:n], ALU.pow).then_inc(s[out_sem], 1)

            def constants():
                pool.memset(m12[:, :, :].bitcast(fp32), 0.0).then_inc(s["pool_consts"], 1)
                pool.memset(vparts[:, :, :, 0:1], 1.0).then_inc(s["pool_consts"], 1)
                pool.memset(maskrow[:, 0, :], 1.0).then_inc(s["pool_consts"], 1)
                pool.wait_ge(s["pool_consts"], 4)
                pool.memset(kst[3 * HD:3 * HD + 3, :, :].bitcast(fp32), 1.0).then_inc(s["pool_consts"], 1)
                pool.wait_ge(s["pool_consts"], 5)
                small(maskcol_raw[:, :], mask.rearrange("b (c p) -> p (b c)", p=P), "small_loaded")
                small(vb_bc[:, :], repeated(v_b), "small_loaded")
                small(cb_bc[:, :], repeated(c_b), "small_loaded")
                split_weight_lo(3)
                for dst, src in ((cols[:, LN2W:LN2W + KT], ln2_w), (cols[:, LN2B:LN2B + KT], ln2_b),
                                 (cols[:, FCB:FCB + FT], fc_b)):
                    small(dst, column(src), "mlp_columns_loaded")

            def split_weight_lo(n):
                pool.wait_ge(s["w_hi_act"], n - 1)
                pool.tensor_tensor(w_att[:, n, 1, :, :], w_att_raw[:, n, 1, :, :], w_att[:, n, 0, :, :].bitcast(fp32),
                                   ALU.subtract).then_inc(s["w_lo_pool"], 1)

            def step(it, g):
                G = it * NG + g
                for u in range(4):
                    if u == 2 and g == 2 and batch(it + 2):
                        inverse_std(it + 2, TT, "ln_var", "ln_rstd")
                    if u == 2 and g == 0 and batch(it - 1):
                        b = it - 1
                        wait(pool, "pv_taken", (b + 1) * 16)
                        for t in range(TT):
                            a = att[:, t, :].rearrange("p (h d) -> p h d", h=H)
                            pool.tensor_tensor(a, a, rl[:, t, :].rearrange("p (h o) -> p h o", o=1).to_broadcast([P, H, HD]),
                                               ALU.mult).then_inc(s["att_normed"], 1)
                    if group(G):
                        wait(pool, "p_hi_done", (G * 4) + (u + 1))
                        wait(pool, "pv_mm", (G - 1) * 2)
                        slot = (g % 2) * 4 + u
                        pool.tensor_tensor(p_lo[:, slot, :], p32[:, u % 2, :], p_hi[:, slot, :],
                                           ALU.subtract).then_inc(s["p_lo_done"], 1)
                if g == 1 and batch(it + 1):
                    b = it + 1
                    wait(pool, "x_normed", (b + 1) * 2)
                    wait(pool, "small_loaded", SMALL)
                    for t in range(TT):
                        h = hidden_tile(b * TT + t)
                        pool.tensor_tensor(h, h, cb_bc[:, :], ALU.add).then_inc(s["cb_added"], 1)

            def ln2(j):
                inverse_std(j, 1, "y_var", "y_rstd")

            def tail(it, g):
                if it == B - 1:
                    ln2(g)

            iterations(pool, step, constants, tail)

            def pb(j):
                wait(pool, "y_normed", j + 1)
                h = hidden_tile(j)
                pool.tensor_tensor(h, h, pb_bc[:, :], ALU.add).then_inc(s["pb_added"], 1)

            pool.wait_ge(s["pb_loaded"], 16)
            for t in range(CH):
                pb(t)

            def body(c, first):
                if has_next(c):
                    for t in range(CH):
                        ln2(c * CH + (CH + t))
                        pb(c * CH + (CH + t))

            chunks(pool, body)

        @block.scalar
        def _(act):
            def weights():
                act.wait_ge(s["wq_loaded"], 16)
                act.wait_ge(s["wk_loaded"], 16)
                for c in range(NG):
                    for n in range(2):
                        act.activation(w_att[:, n, 0, :, c * P:(c + 1) * P], w_att_raw[:, n, 1, :, c * P:(c + 1) * P],
                                       ACT.Copy).then_inc(s["w_hi_qk"], 1)
                for n, sem in ((2, "wv_loaded"), (3, "wc_loaded")):
                    act.wait_ge(s[sem], 16)
                    act.activation(w_att[:, n, 0, :, :], w_att_raw[:, n, 1, :, :], ACT.Copy).then_inc(s["w_hi_act"], 1)
                act.wait_ge(s["qkb_loaded"], 32)
                act.wait_ge(s["mask_ready"], 3)
                act.activation(maskbias[:, :], maskcol[:, 0:KC], ACT.Copy).then_inc(s["maskbias_ready"], 1)

            def exps(it, g, u):
                G = it * NG + g
                if not group(G):
                    return
                kc = u % KC
                n = G * 4 + u
                wait(act, "st_mm", n + 1)
                wait(act, "p_lo_done", n - 1)
                act.activation(p32[:, u % 2, :], psum[:, ST + kc, :], ACT.Exp, bias=maskbias[:, kc:kc + 1], scale=SCALE32)
                wait(act, "pv_mm", (G - 1) * 2)
                act.activation(p_hi[:, (g % 2) * 4 + u, :], psum[:, ST + kc, :], ACT.Exp, bias=maskbias[:, kc:kc + 1],
                               scale=SCALE32).then_inc(s["p_hi_done"], 1)

            def context_hi(it, j):
                b = it + 1
                wait(act, "ctx_tr", b * 2 + (j + 1))
                act.activation(cs[:, 0, 2 * j:2 * j + 2, :], in_bank("ctx", j).rearrange("p (k q) -> p k q", k=2),
                               ACT.Copy).then_inc(s["ctx_hi_done"], 1)

            def values_cast(b, part):
                wait(act, "v_added", (b + 1) * 2)
                wait(act, "pv_mm", b * 8)
                if part:
                    wait(act, "v_rest", b + 1)
                lo = 1 + HD * part
                act.activation(vparts[:, :, :, lo:lo + HD], v32[:, :, :].rearrange("p c (h d) -> p c h d", h=H),
                               ACT.Copy).then_inc(s["v_cast"], 1)

            def qk_high(it, g):
                G = it * NG + g + 3
                if group(G):
                    wait(act, "qk_proj", G + 1)
                    wait(act, "qk_stored", G * 16)
                    for n, col in ((0, QB), (1, KB_)):
                        act.activation(qk[:, 1 + n, :], in_bank("qk", g)[:, n * LQ:(n + 1) * LQ], ACT.Identity,
                                       bias=cols[:, col + (g + 3) % NG:col + (g + 3) % NG + 1]).then_inc(s["qk_hi_done"], 1)

            def maxima_out(it, g):
                G = it * NG + g + 1
                if group(G):
                    wait(act, "m_tr", G + 1)
                    wait(act, "m_stored", G * 16)
                    act.activation(mrow[:, :], in_bank("m", g)[0:3 * GH, 0:LQ], ACT.Copy).then_inc(s["mrow_ready"], 1)

            def attention_hi(b):
                wait(act, "c_proj", b * 2)
                for j in range(2):
                    wait(act, "att_tr", b * 2 + (j + 1))
                    act.activation(att_t[:, 0, 2 * j:2 * j + 2, :], in_bank("att", j).rearrange("p (k q) -> p k q", k=2),
                                   ACT.Copy).then_inc(s["att_hi_done"], 1)

            def x_hi(b):
                wait(act, "x_affine", (b + 1) * 4)
                act.activation(xs[:, 0, :, :], x_t[:, :, :], ACT.Copy).then_inc(s["x_hi_done"], 1)

            def affine_x(b):
                if isinstance(b, int) and b == 0:
                    act.wait_ge(s["ln1_loaded"], 32)
                wait(act, "x_tr", (b + 1) * 2)
                wait(act, "x_hi_done", b)
                wait(act, "x_lo_done", b)
                for k in range(KT):
                    act.activation(x_t[:, k, :], in_bank("x", k // 2)[:, (k % 2) * LQ:(k % 2 + 1) * LQ], ACT.Identity,
                                   scale=cols[:, LN1W + k:LN1W + k + 1],
                                   bias=cols[:, LN1B + k:LN1B + k + 1]).then_inc(s["x_affine"], 1)

            def mask_columns(b):
                wait(act, "p_hi_done", b * 16)
                cut = slice(b * KC, (b + 1) * KC) if isinstance(b, int) else bass.ds(b * KC, KC)
                act.activation(maskbias[:, :], maskcol[:, cut], ACT.Copy).then_inc(s["maskbias_ready"], 1)

            def step(it, g):
                if g == 0 and batch(it):
                    wait(act, "maskbias_ready", it + 1)
                qk_high(it, g)
                if g == 0:
                    if batch(it + 1):
                        context_hi(it, 0)
                    exps(it, g, 0)
                    if batch(it + 1):
                        context_hi(it, 1)
                    exps(it, g, 1)
                    maxima_out(it, g)
                    if batch(it + 1):
                        x_hi(it + 1)
                    if batch(it):
                        values_cast(it, 0)
                if g == 1:
                    exps(it, g, 0)
                    maxima_out(it, g)
                    if batch(it - 1):
                        attention_hi(it - 1)
                    exps(it, g, 1)
                if g == 2:
                    exps(it, g, 0)
                    exps(it, g, 1)
                    maxima_out(it, g)
                if g == 3:
                    exps(it, g, 0)
                    exps(it, g, 1)
                    maxima_out(it, g)
                exps(it, g, 2)
                if g == 3 and batch(it + 2):
                    affine_x(it + 2)
                exps(it, g, 3)
                if g == 0 and batch(it):
                    values_cast(it, 1)
                if g == 3 and batch(it + 1) and not (isinstance(it, int) and it == -1):
                    mask_columns(it + 1)

            def affine(c, j, t):
                wait(act, "y_tr", j + 1)
                wait(act, "y_lo_done", (j - t))
                for k in range(KT):
                    act.activation(y_t[:, k, t * P:(t + 1) * P], turned(c, t)[:, k * P:(k + 1) * P], ACT.Identity,
                                   scale=cols[:, LN2W + k:LN2W + k + 1],
                                   bias=cols[:, LN2B + k:LN2B + k + 1]).then_inc(s["y_affine"], 1)

            def gelu(F, f):
                wait(act, "fc_mm", F + 1)
                wait(act, "h_lo_done", F - 1)
                act.activation(h32[:, f % 2, :], psum[:, FC + f % 2, :], ACT.Gelu_apprx_tanh,
                               bias=cols[:, FCB + f:FCB + f + 1]).then_inc(s["h_done"], 1)

            def tail(it, g):
                if it == B - 1 and g == 2:
                    act.wait_ge(s["mlp_columns_loaded"], 3 * 16)
                    wait(act, "x_lo_done", B)
                    wait(act, "qk_stored", GROUPS * 16)
                    affine(0, 0, 0)
                if it == B - 1 and g == 3:
                    affine(0, 1, 1)
                    affine(0, 2, 2)
                if it == B and g == 0:
                    affine(0, 3, 3)
                if it == B and g == 1:
                    wait(act, "v_split", B)
                    gelu(0, 0)

            iterations(act, step, weights, tail)

            def body(c, first):
                for i in range(FT):
                    if i < FT - 1:
                        gelu(c * FT + (i + 1), i + 1)
                    elif has_next(c):
                        gelu(c * FT + FT, 0)
                    if has_next(c) and i % 3 == 0 and 3 <= i <= 12:
                        t = i // 3 - 1
                        affine(c + 1, c * CH + (CH + t), t)

            chunks(act, body)

        @block.vector
        def _(dve):
            def weights_lo():
                for c in range(NG):
                    for n in range(2):
                        dve.wait_ge(s["w_hi_qk"], 2 * c + n + 1)
                        piece = w_att[:, n, :, :, c * P:(c + 1) * P]
                        dve.tensor_tensor(piece[:, 1], w_att_raw[:, n, 1, :, c * P:(c + 1) * P], piece[:, 0].bitcast(fp32),
                                          ALU.subtract).then_inc(s["w_lo_dve"], 1)
                dve.wait_ge(s["w_hi_act"], 1)
                dve.tensor_tensor(w_att[:, 2, 1, :, :], w_att_raw[:, 2, 1, :, :], w_att[:, 2, 0, :, :].bitcast(fp32),
                                  ALU.subtract).then_inc(s["w_lo_dve"], 1)
                dve.wait_ge(s["small_loaded"], SMALL)
                dve.tensor_scalar(maskrow[:, 1, :], mrow_raw[:, :], MASKED, -MASKED, ALU.mult, ALU.add).then_inc(s["mask_ready"], 1)
                dve.tensor_scalar(maskcol[:, :], maskcol_raw[:, :], SCALE32 * MASKED, -SCALE32 * MASKED,
                                  ALU.mult, ALU.add).then_inc(s["mask_ready"], 1)
                dve.wait_ge(s["mask_ready"], 2)
                dve.tensor_scalar_add(maskcol[:, :], maskcol[:, :], PSHIFT).then_inc(s["mask_ready"], 1)

            def maximum(it, g, heads):
                G = it * NG + g + 2
                if not group(G):
                    return
                if heads[0] == 0:
                    wait(dve, "m_lo_done", G)
                for h in heads:
                    n = G * 4 + h
                    wait(dve, "max_mm", n + 1)
                    dve.tensor_reduce(out=negm[:, :, h:h + 1], in_=psum[:, MX + h % 2, :].rearrange("p (t k) -> p t k", t=TT),
                                      axis=AX.X, op=ALU.max, negate=True).then_inc(s["max_taken"], 1)
                if heads[-1] == GH - 1:
                    wait(dve, "max_taken", (G + 1) * 4)
                    wait(dve, "m_tr", G)
                    dve.tensor_copy(m12[:, :, GH:2 * GH], negm[:, :, :]).then_inc(s["m_hi_done"], 1)
                    wait(dve, "m_hi_done", G + 1)
                    dve.tensor_tensor(m12[:, :, 2 * GH:3 * GH], negm[:, :, :], m12[:, :, GH:2 * GH].bitcast(fp32),
                                      ALU.subtract).then_inc(s["m_lo_done"], 1)

            def statistics(b, tiles, stats_sem, mv_sem, var_sem):
                n = len(tiles)
                for t, j in enumerate(tiles):
                    dve.bn_stats(stats[:, t, :], hidden_tile(j)).then_inc(s[stats_sem], 1)
                wait(dve, stats_sem, (b + 1) * n)
                dve.memset(scratch[:, :], 0.0)
                for t in range(n):
                    dve.bn_aggr(mv[:, t, :], stats[:, t, :]).then_inc(s[mv_sem], 1)
                wait(dve, mv_sem, (b + 1) * n)
                dve.tensor_scalar_add(vareps[:, 0:n], mv[:, 0:n, 1], EPS).then_inc(s[var_sem], 1)

            def add_hidden(it, t):
                b = it - 1 - t
                wait(dve, "c_proj", b * 2 + (t + 1))
                wait(dve, "cb_added", (b + 1) * 2)
                h = hidden_tile(b * TT + t)
                dve.tensor_tensor(h, in_bank("c", t), h, ALU.add).then_inc(s["hidden_added"], 1)

            def add_values(it, t):
                b = it + 1
                wait(dve, "v_proj", b * 2 + (t + 1))
                wait(dve, "v_split", b)
                dve.tensor_tensor(v32[:, t, :], in_bank("v", t), vb_bc[:, :], ALU.add).then_inc(s["v_added"], 1)

            def low_parts(it, g):
                G = it * NG + g + 3
                if group(G):
                    wait(dve, "qk_hi_done", (G + 1) * 2)
                    for n, col in ((0, QB), (1, KB_)):
                        piece = slice(n * LQ, (n + 1) * LQ)
                        dve.scalar_tensor_tensor(out=qk[:, 3 * n, :], in0=in_bank("qk", g)[:, piece],
                                                 scalar=cols[:, col + (g + 3) % NG:col + (g + 3) % NG + 1],
                                                 in1=qk[:, 1 + n, :].bitcast(fp32), op0=ALU.add,
                                                 op1=ALU.subtract).then_inc(s["qk_lo_done"], 1)

            v_heads = v32[:, :, :].rearrange("p c (h d) -> p c h d", h=H)

            def context_lo(it, j):
                b = it + 1
                wait(dve, "ctx_hi_done", b * 2 + (j + 1))
                dve.tensor_tensor(cs[:, 1, 2 * j:2 * j + 2, :], in_bank("ctx", j).rearrange("p (k q) -> p k q", k=2),
                                  cs[:, 0, 2 * j:2 * j + 2, :].bitcast(fp32), ALU.subtract).then_inc(s["ctx_lo_done"], 1)

            def products_out(it, g):
                G = it * NG + g - 1
                if not group(G):
                    return
                if (g - 1) % NG == 0:
                    wait(dve, "att_tr", it * 2)
                for t in range(TT):
                    wait(dve, "pv_mm", G * 2 + (t + 1))
                    rows = psum[:, PV + t, 0:GH * VW].rearrange("p (h c) -> p h c", c=VW)
                    h0 = GH * ((g - 1) % NG)
                    dve.tensor_reduce(out=att[:, t, h0 * HD:(h0 + GH) * HD].rearrange("p (h d) -> p h d", h=GH),
                                      in_=rows[:, :, 1:VW].rearrange("p h (s d) -> p h d s", s=3),
                                      axis=AX.X, op=ALU.add).then_inc(s["pv_taken"], 1)
                    dve.reciprocal(rl[:, t, h0:h0 + GH], rows[:, :, 0]).then_inc(s["pv_taken"], 1)

            def step(it, g):
                if isinstance(it, int) and it == B and g == 0:
                    ln2_norm(CH - 1, CH - 1)
                low_parts(it, g)
                if g == 0 and batch(it + 1):
                    context_lo(it, 0)
                    context_lo(it, 1)
                if g == 3 and batch(it + 2):
                    b = it + 2
                    wait(dve, "ln_rstd", b + 1)
                    wait(dve, "x_tr", b * 2)
                    wait(dve, "x_hi_done", b)
                    wait(dve, "x_lo_done", b)
                    for t in range(TT):
                        dve.tensor_scalar(xn[:, t, :], hidden_tile(b * TT + t), mv[:, t, 0:1], rstd[:, t:t + 1],
                                          ALU.subtract, ALU.mult).then_inc(s["x_normed"], 1)
                if g != 1:
                    products_out(it, g)
                maximum(it, g, (0, 1))
                if g == 0 and batch(it + 1):
                    wait(dve, "x_hi_done", it + 2)
                    dve.tensor_tensor(xs[:, 1, :, :], x_t[:, :, :], xs[:, 0, :, :].bitcast(fp32),
                                      ALU.subtract).then_inc(s["x_lo_done"], 1)
                if g == 0 and batch(it):
                    wait(dve, "v_cast", it * 2 + 1)
                    for kc in range(KC):
                        ins = dve.tensor_tensor(v_heads[:, kc], v_heads[:, kc], vparts[:, kc, :, 1:1 + HD], ALU.subtract)
                    ins.then_inc(s["v_rest"], 1)
                if g == 1 and batch(it - 1):
                    b = it - 1
                    for j in range(2):
                        wait(dve, "att_hi_done", b * 2 + (j + 1))
                        dve.tensor_tensor(att_t[:, 1, 2 * j:2 * j + 2, :], in_bank("att", j).rearrange("p (k q) -> p k q", k=2),
                                          att_t[:, 0, 2 * j:2 * j + 2, :].bitcast(fp32), ALU.subtract).then_inc(s["att_lo_done"], 1)
                if g == 1:
                    products_out(it, g)
                if g == 2 and batch(it + 2):
                    b = it + 2
                    wait(dve, "x_loaded", (b + 1) * 16)
                    wait(dve, "ln_rstd", b)
                    wait(dve, "x_normed", b * 2)
                    statistics(b, [b * TT + t for t in range(TT)], "ln_stats", "ln_mv", "ln_var")
                if g in (1, 2) and batch(it + 1):
                    add_values(it, g - 1)
                if g == 0 and batch(it - 2):
                    add_hidden(it, 1)
                if g == 3 and batch(it - 1):
                    add_hidden(it, 0)
                maximum(it, g, (2, 3))
                if g == 0 and batch(it):
                    wait(dve, "v_cast", it * 2 + 2)
                    for kc in range(KC):
                        ins = dve.tensor_tensor(vparts[:, kc, :, 1 + 2 * HD:VW], v_heads[:, kc],
                                                vparts[:, kc, :, 1 + HD:1 + 2 * HD], ALU.subtract)
                    ins.then_inc(s["v_split"], 1)

            def weights(i):
                dve.wait_ge(w2_loaded[i], 32)
                dve.tensor_copy(w_mlp[i][:, 0::2, :], w_mlp_raw[i][:, 1::2, :]).then_inc(s["w2_hi"], 1)
                dve.wait_ge(s["w2_hi"], i + 1)
                dve.tensor_tensor(w_mlp[i][:, 1::2, :], w_mlp_raw[i][:, 1::2, :], w_mlp[i][:, 0::2, :].bitcast(fp32),
                                  ALU.subtract).then_inc(s["w2_lo"], 1)

            def ln2_stats(j):
                wait(dve, "y_rstd", j)
                wait(dve, "y_normed", j)
                statistics(j, [j], "y_stats", "y_mv", "y_var")

            def ln2_norm(j, t):
                wait(dve, "y_rstd", j + 1)
                wait(dve, "y_tr", j - 1)
                dve.tensor_scalar(yn[:, t % 2, :], hidden_tile(j), mv[:, 0, 0:1], rstd[:, 0:1],
                                  ALU.subtract, ALU.mult).then_inc(s["y_normed"], 1)

            def split_y(c):
                wait(dve, "y_affine", (c + 1) * CH * KT)
                wait(dve, "fc_mm", c * FT)
                for k in range(KT):
                    dve.tensor_copy(y_hi[:, k, :], y_t[:, k, :]).then_inc(s["y_hi_done"], 1)
                    wait(dve, "y_hi_done", c * KT + (k + 1))
                    dve.tensor_tensor(y_lo[:, k, :], y_t[:, k, :], y_hi[:, k, :].bitcast(fp32),
                                      ALU.subtract).then_inc(s["y_lo_done"], 1)

            def split_h(F, f):
                wait(dve, "h_done", F + 1)
                wait(dve, "proj_mm", F - 1)
                dve.tensor_copy(h_hi[:, f % 2, :], h32[:, f % 2, :]).then_inc(s["h_hi_done"], 1)
                wait(dve, "h_hi_done", F + 1)
                dve.tensor_tensor(h_lo[:, f % 2, :], h32[:, f % 2, :], h_hi[:, f % 2, :].bitcast(fp32),
                                  ALU.subtract).then_inc(s["h_lo_done"], 1)

            def tail(it, g):
                if it == B - 1:
                    if g == 0:
                        wait(dve, "hidden_added", CH)
                        wait(dve, "ln_rstd", B)
                        wait(dve, "x_normed", B * 2)
                    else:
                        ln2_norm(g - 1, g - 1)
                    ln2_stats(g)
                    if g >= 2:
                        weights(g - 2)
                if it == B and g == 0:
                    split_y(0)
                if it == B and g == 1:
                    weights(2)
                    wait(dve, "att_tr", B * 2)
                    split_h(0, 0)
                    weights(3)

            iterations(dve, step, weights_lo, tail)

            def add_out(c):
                wait(dve, "proj_mm", (c + 1) * FT)
                for t in range(CH):
                    wait(dve, "pb_added", c * CH + (t + 1))
                    h = hidden_tile(c * CH + t)
                    dve.tensor_tensor(h, psum[:, ACC[t], :], h, ALU.add).then_inc(s["out_added"], 1)

            wait(dve, "hidden_added", B * 2)

            def body(c, first):
                for i in range(FT):
                    if i == 0 and not first:
                        add_out(c - 1)
                    if first and i + 4 < FT:
                        weights(i + 4)
                    if i < FT - 1:
                        split_h(c * FT + (i + 1), i + 1)
                    elif has_next(c):
                        split_y(c + 1)
                        split_h(c * FT + FT, 0)
                    if has_next(c):
                        for t in range(CH):
                            if i == 3 * t + 1:
                                ln2_stats(c * CH + (CH + t))
                            if i == 3 * t + 2:
                                ln2_norm(c * CH + (CH + t), t)

            chunks(dve, body)
            add_out(CHUNKS - 1)

        @block.tensor
        def _(pe):
            def three_passes(out_ap, pairs, last_sem=None):
                n = len(pairs)
                for i, (a_hi, a_lo, b_hi, b_lo) in enumerate(pairs):
                    nc.tensor.matmul(out_ap, a_hi, b_hi, start=(i == 0), stop=False)
                    nc.tensor.matmul(out_ap, a_hi, b_lo, start=False, stop=False)
                    ins = nc.tensor.matmul(out_ap, a_lo, b_hi, start=False, stop=(i == n - 1))
                return ins

            pe.wait_ge(s["ident_ready"], 1)

            def transposed_scores(it, g, pair):
                G = it * NG + g
                if not group(G):
                    return
                if pair == 0:
                    wait(pe, "m_stored", (G + 1) * 16)
                for kc in range(KC):
                    n = G * 4 + 2 * pair + kc
                    wait(pe, "p_hi_done", n - 1)
                    for hh in range(2):
                        h = GH * g + 2 * pair + hh
                        ins = nc.tensor.matmul(psum[:, ST + kc, hh * LQ:(hh + 1) * LQ],
                                               kst[0:SUBROWS, h, kc * P:(kc + 1) * P], qst[0:SUBROWS, h, :],
                                               start=True, stop=True)
                    ins.then_inc(s["st_mm"], 1)

            def scores(it, g, heads):
                G = it * NG + g + 2
                if not group(G):
                    return
                if heads[0] == 0:
                    wait(pe, stack_filled[g % 2], fills_upto(G, g % 2))
                    wait(pe, "pool_consts", 5)
                for hh in heads:
                    h = GH * ((g + 2) % NG) + hh
                    wait(pe, "max_taken", G * 4 + (hh - 1))
                    for t in range(TT):
                        ins = nc.tensor.matmul(psum[:, MX + hh % 2, t * LK:(t + 1) * LK],
                                               qst[0:MAXROWS, h, t * P:(t + 1) * P], kst[0:MAXROWS, h, :],
                                               start=True, stop=True)
                    ins.then_inc(s["max_mm"], 1)

            def project_qk(it, g):
                G = it * NG + g + 3
                if not group(G):
                    return
                b = it if g == 0 else it + 1
                wait(pe, "ctx_lo_done", (b + 1) * 2)
                wait(pe, "x_lo_done", b + 1)
                if isinstance(it, int) and it == -1:
                    pe.wait_ge(s["w_lo_dve"], 2 * G + 2)
                elif isinstance(it, int) and it == 0 and g == 0:
                    pe.wait_ge(s["w_lo_dve"], 2 * NG)
                bank = bank_of(it, "qk", g)
                c0 = P * ((g + 3) % NG)
                for n, src in ((0, xs), (1, cs)):
                    ins = three_passes(bank[:, n * LQ:(n + 1) * LQ],
                                       [(w_att[:, n, 0, k, c0:c0 + P], w_att[:, n, 1, k, c0:c0 + P],
                                         src[:, 0, k, :], src[:, 1, k, :]) for k in range(KT)])
                ins.then_inc(s["qk_proj"], 1)

            def project_v(it, t):
                if not batch(it + 1):
                    return
                wait(pe, "w_lo_dve", 2 * NG + 1)
                bank = bank_of(it, "v", t)
                three_passes(bank, [(cs[:, 0, k, t * P:(t + 1) * P], cs[:, 1, k, t * P:(t + 1) * P],
                                     w_att[:, 2, 0, k, :], w_att[:, 2, 1, k, :]) for k in range(KT)]).then_inc(s["v_proj"], 1)

            def project_c(it, t):
                b = it - 1 - t
                if not batch(b):
                    return
                wait(pe, "att_lo_done", (b + 1) * 2)
                wait(pe, "w_lo_pool", 1)
                bank = bank_of(it, "c", t)
                three_passes(bank, [(att_t[:, 0, k, t * P:(t + 1) * P], att_t[:, 1, k, t * P:(t + 1) * P],
                                     w_att[:, 3, 0, k, :], w_att[:, 3, 1, k, :]) for k in range(KT)]).then_inc(s["c_proj"], 1)

            def transposes(it, kind, j, b, src, ready, per_batch, done):
                if not batch(b):
                    return
                wait(pe, ready, (b + 1) * per_batch)
                bank = bank_of(it, kind, j)
                for i in range(2):
                    for t in range(TT):
                        k = 2 * j + i
                        ins = nc.tensor.transpose(bank[:, i * LQ + t * P:i * LQ + (t + 1) * P],
                                                  src[:, t, k * P:(k + 1) * P], ident[:, :])
                ins.then_inc(s[done], 1)

            def values(it, g):
                G = it * NG + g - 1
                if not group(G):
                    return
                b = it - 1 if g == 0 else it
                wait(pe, "p_lo_done", (G + 1) * 4)
                wait(pe, "v_split", b + 1)
                gp = (g - 1) % NG
                for t in range(TT):
                    wait(pe, "pv_taken", (G - 1) * 4 + (2 * t + 2))
                    for hh in range(GH):
                        o = psum[:, PV + t, hh * VW:(hh + 1) * VW]
                        for kc in range(KC):
                            slot = (gp % 2) * 4 + (hh // 2) * 2 + kc
                            cut = slice((hh % 2) * LQ + t * P, (hh % 2) * LQ + (t + 1) * P)
                            nc.tensor.matmul(o, p_hi[:, slot, cut], vparts[:, kc, GH * gp + hh, :],
                                             start=(kc == 0), stop=False)
                            ins = nc.tensor.matmul(o[:, 0:VW_LO], p_lo[:, slot, cut], vparts[:, kc, GH * gp + hh, 0:VW_LO],
                                                   start=False, stop=(kc == KC - 1))
                    ins.then_inc(s["pv_mm"], 1)

            def transpose_max(it, g):
                G = it * NG + g + 1
                if not group(G):
                    return
                wait(pe, "m_lo_done", G + 1)
                bank = bank_of(it, "m", g)
                for t in range(TT):
                    ins = nc.tensor.transpose(bank[0:3 * GH, t * P:(t + 1) * P], m12[:, t, :].bitcast(fp32), ident[:, :])
                ins.then_inc(s["m_tr"], 1)

            def step(it, g):
                if isinstance(it, int) and it == B and g == 0:
                    transpose_y(0, CH - 1, CH - 1)
                project_qk(it, g)
                transposed_scores(it, g, 0)
                if g == 0:
                    transposes(it, "ctx", 0, it + 1, ctx_sb, "ctx_loaded", 16, "ctx_tr")
                    values(it, g)
                    transposes(it, "ctx", 1, it + 1, ctx_sb, "ctx_loaded", 16, "ctx_tr")
                    scores(it, g, (0, 1))
                    transpose_max(it, g)
                    project_c(it, 1)
                if g == 1:
                    transpose_max(it, g)
                    scores(it, g, (0, 1))
                    for j in range(2):
                        transposes(it, "att", j, it - 1, att, "att_normed", 2, "att_tr")
                    values(it, g)
                    project_v(it, 0)
                if g == 2:
                    transpose_max(it, g)
                    values(it, g)
                    scores(it, g, (0, 1))
                    project_v(it, 1)
                if g == 3:
                    transpose_max(it, g)
                    values(it, g)
                    scores(it, g, (0, 1))
                    project_c(it, 0)
                    transposes(it, "x", 0, it + 2, xn, "x_normed", 2, "x_tr")
                transposed_scores(it, g, 1)
                if g == 3:
                    transposes(it, "x", 1, it + 2, xn, "x_normed", 2, "x_tr")
                scores(it, g, (2, 3))

            def fc(c, F, f):
                wait(pe, "w2_lo", f + 1)
                wait(pe, "h_done", F - 1)
                for k in range(KT):
                    wait(pe, "y_lo_done", c * KT + (k + 1))
                    w = w_mlp[f][:, :, k * P:(k + 1) * P]
                    bank = psum[:, FC + f % 2, :]
                    nc.tensor.matmul(bank, w[:, 0, :], y_hi[:, k, :], start=(k == 0), stop=False)
                    nc.tensor.matmul(bank, w[:, 0, :], y_lo[:, k, :], start=False, stop=False)
                    ins = nc.tensor.matmul(bank, w[:, 1, :], y_hi[:, k, :], start=False, stop=(k == KT - 1))
                ins.then_inc(s["fc_mm"], 1)

            def proj(c, F, f):
                wait(pe, "h_lo_done", F + 1)
                if isinstance(F, int) and F == 0:
                    wait(pe, "p_hi_done", GROUPS * 4)
                    wait(pe, "hidden_added", B * 2)
                for t in range(CH):
                    if f == 0:
                        wait(pe, "out_added", (c - 1) * CH + (t + 1))
                    cut = slice(t * P, (t + 1) * P)
                    acc = psum[:, ACC[t], :]
                    nc.tensor.matmul(acc, h_hi[:, f % 2, cut], w_mlp[f][:, 2, :], start=(f == 0), stop=False)
                    nc.tensor.matmul(acc, h_hi[:, f % 2, cut], w_mlp[f][:, 3, :], start=False, stop=False)
                    ins = nc.tensor.matmul(acc, h_lo[:, f % 2, cut], w_mlp[f][:, 2, :], start=False, stop=(f == FT - 1))
                ins.then_inc(s["proj_mm"], 1)

            def transpose_y(c, j, t):
                wait(pe, "y_normed", j + 1)
                wait(pe, "y_affine", (j - 1) * KT)
                for k in range(KT):
                    ins = nc.tensor.transpose(turned(c, t)[:, k * P:(k + 1) * P], yn[:, t % 2, k * P:(k + 1) * P], ident[:, :])
                ins.then_inc(s["y_tr"], 1)

            def tail(it, g):
                if it == B - 1 and g == 2:
                    wait(pe, "max_taken", GROUPS * 4)
                    transpose_y(0, 0, 0)
                if it == B - 1 and g == 3:
                    transpose_y(0, 1, 1)
                    transpose_y(0, 2, 2)
                if it == B and g == 1:
                    fc(0, 0, 0)

            iterations(pe, step, tail=tail)

            def body(c, first):
                for i in range(FT):
                    if i < FT - 1:
                        fc(c, c * FT + (i + 1), i + 1)
                    elif has_next(c):
                        fc(c + 1, c * FT + FT, 0)
                    if has_next(c) and i % 3 == 0 and 3 <= i <= 12:
                        t = i // 3 - 1
                        transpose_y(c + 1, c * CH + (CH + t), t)
                    proj(c, c * FT + i, i)

            chunks(pe, body)


def mybir_f32(v):
    import numpy as np
    return np.float32(v)


_INS = ["x", "ctx_2048", "mask_BxS2_bf1"] + ["L0_xattn_" + n for n in (
    "ln1_w", "ln1_b", "q_w", "q_b", "k_w", "k_b", "v_w", "v_b", "cproj_w", "cproj_b",
    "ln2_w", "ln2_b", "fc_w", "fc_b", "proj_w", "proj_b")]
_OUTS = [((8, 256, 512), "float32")]


def kernel(**inputs):
    import numpy as _np
    import concourse.bacc as _bacc
    from concourse import mybir as _mybir
    from concourse.bass_utils import run_bass_kernel_spmd as _run

    nc = _bacc.Bacc("TRN2", target_bir_lowering=False, num_devices=1)
    arrays, args = {}, []
    for name in _INS:
        a = _np.ascontiguousarray(inputs[name])
        if a.dtype == _np.bool_:
            a = a.view(_np.uint8)
        arrays[f"in_{name}_dram"] = a
        args.append(nc.dram_tensor(f"in_{name}_dram", a.shape, _mybir.dt.from_np(a.dtype), kind="ExternalInput").ap())
    for i, (shape, dtype) in enumerate(_OUTS):
        dt = _mybir.dt.from_np(_np.dtype(dtype))
        args.append(nc.dram_tensor(f"out_{i}_dram", shape, dt, kind="ExternalOutput").ap())
    xattn_kernel(nc, *args)
    r = _run(nc, [arrays], core_ids=[0])
    got = tuple(r.results[0][f"out_{i}_dram"] for i in range(len(_OUTS)))
    return got[0]
```

```python
import numpy as np
import concourse.bass as bass
from concourse import mybir
from contextlib import ExitStack

fp32 = mybir.dt.float32
fp32r = mybir.dt.float32r
bf16 = mybir.dt.bfloat16
fp16 = mybir.dt.float16
u8 = mybir.dt.uint8
ALU = mybir.AluOpType
ACT = mybir.ActivationFunctionType
AX = mybir.AxisListType


def xattn_kernel(nc, x, ctx_in, mask, ln1_w, ln1_b, q_w, q_b, k_w, k_b, v_w, v_b, c_w, c_b,
                 ln2_w, ln2_b, fc_w, fc_b, proj_w, proj_b, out):
    B, LQ, D = x.shape
    LK = ctx_in.shape[1]
    H, HD = 16, 32
    INNER = fc_w.shape[1]
    P = 128
    KT = D // P
    TT = LQ // P
    KC = LK // P
    GH = P // HD
    NG = H // GH
    GROUPS = B * NG
    FT = INNER // P
    CH = 4
    CW = CH * P
    CHUNKS = B * LQ // CW
    VW = 1 + 3 * HD
    VW_LO = 1 + 2 * HD
    SCALE = float(HD) ** -0.5
    EPS = 1e-5
    PSHIFT = 7.5
    MASKED = float(2.0 ** 127)
    MAXROWS = 3 * HD + 1
    SUBROWS = 3 * HD + 3
    SCALE32 = float(np.float32(SCALE))

    ctx = ExitStack()
    with ctx:
        def sb(name, shape, dt, offset):
            return nc.alloc_sbuf_tensor_at(name, shape, dt, offset=offset)

        BASE = 16512
        KB = 1024
        hidden = sb("hidden", [P, B * TT, D], fp32, BASE)
        C0 = BASE + 32 * KB
        ident = sb("ident", [P, P], fp32, C0)
        cols = sb("cols", [P, 6 * KT + FT], fp32, C0 + 512)
        maskcol = sb("maskcol", [P, B * KC], fp32, C0 + 704)
        maskcol_raw = sb("maskcol_raw", [P, B * KC], u8, C0 + 768)
        stats = sb("stats", [P, 2, 6], fp32, C0 + 800)
        mv = sb("mv", [P, 2, 2], fp32, C0 + 864)
        rstd = sb("rstd", [P, 2], fp32, C0 + 896)
        mhalf = sb("mhalf", [P, 2], fp32, C0 + 928)
        vareps = sb("vareps", [P, 2], fp32, C0 + 960)
        maskbias = sb("maskbias", [P, KC], fp32, C0 + 992)
        scratch = sb("scratch", [P, 1], fp32, C0 + 1024)
        act_scratch = sb("act_scratch", [P, 1], fp32, C0 + 672)
        R0 = C0 + 1056

        w_att = sb("w_att", [P, 4, 2, KT, D], fp32r, R0)
        w_att_raw = sb("w_att_raw", [P, 4, 2, KT, D], fp32, R0)
        A1 = R0 + 64 * KB
        stacks = sb("stacks", [P, H, 2, LQ], fp32r, A1)
        qst, kst = stacks[:, :, 0], stacks[:, :, 1]
        A2 = A1 + 32 * KB
        att_t = sb("att_t", [P, 2, KT, LQ], fp32r, A2)
        p32 = sb("p32", [P, 2, 2 * LQ], fp32, A2 + 8 * KB)
        p_hi = sb("p_hi", [P, 8, 2 * LQ], fp16, A2 + 12 * KB)
        p_lo = sb("p_lo", [P, 8, 2 * LQ], fp16, A2 + 20 * KB)
        vparts = sb("vparts", [P, KC, H, VW], bf16, A2 + 28 * KB)
        A3 = R0 + 131 * KB
        xs = sb("xs", [P, 2, KT, LQ], fp32r, A3)
        cs = sb("cs", [P, 2, KT, LK], fp32r, A3 + 8 * KB)
        ctx_sb = sb("ctx_sb", [P, KC, D], fp32, A3 + 16 * KB)
        xn = sb("xn", [P, 2, TT, D // 2], fp32, A3 + 20 * KB)
        x_t = sb("x_t", [P, KT, LQ], fp32, A3 + 20 * KB)
        qk = sb("qk", [P, 4, LQ], fp32r, A3 + 24 * KB)
        v32 = sb("v32", [P, KC, D], fp32, A3 + 28 * KB)
        A4 = A3 + 32 * KB
        att = sb("att", [P, TT, D], fp32, A4)
        vb_bc = sb("vb_bc", [P, D], fp32, A4 + 4 * KB)
        cb_bc = sb("cb_bc", [P, D], fp32, A4 + 6 * KB)
        A5 = A4 + 8 * KB
        negm = sb("negm", [P, TT, GH], fp32, A5)
        m12 = sb("m12", [P, TT, 3 * GH], fp32r, A5 + 32)
        rl = sb("rl", [P, TT, H], fp32, A5 + 160)
        mrow = sb("mrow", [3 * GH, LQ], fp32r, A5 + 288)
        mrow_raw = sb("maskrow_raw", [B, LK], u8, A5 + 288 + KB)
        v1 = sb("v1", [P, KC, D], bf16, A5 + 544 + KB)
        maskrow = sb("maskrow", [B, 2, LK], fp32, A5 + 544 + KB)
        w_mlp = [sb(f"w_mlp{i}", [P, 4, D], fp32r, R0 + 8 * KB * i) for i in range(FT)]
        w_mlp_raw = [sb(f"w_mlp_raw{i}", [P, 4, D], fp32, R0 + 8 * KB * i) for i in range(FT)]
        y_hi = sb("y_hi", [P, KT, CW], fp32r, A3)
        y_lo = sb("y_lo", [P, KT, CW], fp32r, A3 + 8 * KB)
        yn = sb("yn", [P, 2, D], fp32, A3 + 16 * KB)
        y_t = sb("y_t", [P, KT, CW], fp32, A3 + 20 * KB)
        h32 = sb("h32", [P, 2, CW], fp32, A3 + 28 * KB)
        h_hi = sb("h_hi", [P, 2, CW], fp32r, A3 + 32 * KB)
        h_lo = sb("h_lo", [P, 2, CW], fp32r, A3 + 36 * KB)
        pb_bc = sb("pb_bc", [P, D], fp32, A3 + 40 * KB)
        assert A3 + 42 * KB <= 229344 and A5 + 544 + 3 * KB <= 229344

        mask_rows = nc.dram_tensor("mask_rows", [B, 2, LK], fp32, kind="Internal").ap()
        qk_rows = nc.dram_tensor("qk_rows", [2, HD, GH, 4, LQ], fp32, kind="Internal").ap()

        LN1W, LN1B, QB, KB_, LN2W, LN2B, FCB = [KT * i for i in range(7)]

        psum = ctx.enter_context(nc.psum_tensor("psum", [P, 8, 512], fp32))
        ST, MX, PV, MS = 0, 2, 4, 6
        ACC, FC, TR = (0, 1, 6, 7), 2, 4

        def turned(c, t):
            return psum[:, (FC if isinstance(c, int) and c == 0 else TR) + t % 2, :]

        names = """x_loaded ctx_loaded ln1_loaded qkb_loaded small_loaded mlp_columns_loaded mask_stored out_stored
            ident_zero ident_ready pool_consts mask_ready maskbias_ready
            maskrow_loaded maskcol_loaded wv_loaded wc_loaded w_hi_qk w_hi_act w_lo_dve w_lo_v w_lo_pool
            qk_proj x_tr ctx_tr max_mm st_mm pv_mm m_tr att_tr v_proj c_proj
            x_affine_act x_affine_dve qk_hi_done qk_lo_done p_hi_done p_lo_done mrow_ready att_hi_done att_lo_done
            v1_cast v_cast v_rest v_split v_added max_taken m_hi_done m_lo_done pv_taken att_normed hidden_added
            ln_stats ln_mv ln_var ln_rstd x_normed cb_added x_hi_done x_lo_done ctx_hi_done ctx_lo_done
            qk_stored stack_filled0 stack_filled1 m_stored
            w2_hi w2_lo fc_mm proj_mm y_tr y_affine y_normed y_hi_done y_lo_done h_done h_hi_done h_lo_done
            pb_loaded pb_added out_added y_stats y_mv y_var y_rstd""".split()
        s = {n: ctx.enter_context(nc.semaphore(n)) for n in names}
        wqk_loaded = [ctx.enter_context(nc.semaphore(f"wqk_loaded{c}")) for c in range(NG)]
        w2_loaded = [ctx.enter_context(nc.semaphore(f"w2_loaded{i}")) for i in range(FT)]
        stack_filled = [s["stack_filled0"], s["stack_filled1"]]
        SMALL = 2 * 16
        FILLS = (3 + 1) * 16

        def wait(eng, sem, value):
            if not isinstance(value, int) or value > 0:
                eng.wait_ge(s[sem] if isinstance(sem, str) else sem, value)

        def batch(b):
            return not isinstance(b, int) or 0 <= b < B

        def group(G):
            return not isinstance(G, int) or 0 <= G < GROUPS

        USES = [("qk", 0), ("ctx", 0), ("ctx", 1), ("m", 0), ("c", 1),
                ("qk", 1), ("m", 1), ("att", 0), ("att", 1), ("v", 0),
                ("qk", 2), ("m", 2), ("v", 1),
                ("qk", 3), ("m", 3), ("c", 0), ("x", 0), ("x", 1)]

        def emptied(it, kind, n):
            if kind in ("qk", "m"):
                G = it * NG + n + (3 if kind == "qk" else 1)
                if not group(G):
                    return None
                return ("qk_lo_done", (G + 1) * 2) if kind == "qk" else ("mrow_ready", G + 1)
            b = it + {"v": 1, "att": -1, "c": -1 - n, "x": 2, "ctx": 1}[kind]
            if not batch(b):
                return None
            return {"v": ("v_added", b * 2 + (n + 1)), "att": ("att_lo_done", b * 2 + (n + 1)),
                    "c": ("hidden_added", b * 2 + (n + 1)), "x": (("x_affine_act", "x_affine_dve")[n], b * 2 + 2),
                    "ctx": ("ctx_lo_done", b * 2 + (n + 1))}[kind]

        def bank_of(it, kind, n):
            k = USES.index((kind, n))
            for back in range(k - 2, k - 2 - 2 * len(USES), -2):
                before = emptied(it + back // len(USES), *USES[back % len(USES)])
                if before:
                    wait(nc.tensor, *before)
                    break
            return psum[:, MS + k % 2, :]

        def in_bank(kind, n):
            return psum[:, MS + USES.index((kind, n)) % 2, :]

        def iterations(eng, step, first_weights=None, weights=None, tail=None):
            for g in range(2, NG):
                step(-2, g)
            if first_weights:
                first_weights()
            step(-1, 0)
            if weights:
                weights()
            for g in range(1, NG):
                step(-1, g)
            for it in (0, 1):
                for g in range(NG):
                    step(it, g)
            with eng.Fori(2, B - 2) as it:
                for g in range(NG):
                    step(it, g)
            for it in (B - 2, B - 1, B):
                for g in range(NG):
                    step(it, g)
                    if tail:
                        tail(it, g)
            step(B + 1, 0)

        def chunks(eng, body):
            body(0, True)
            with eng.Fori(1, CHUNKS - 1) as c:
                body(c, False)
            body(CHUNKS - 1, False)

        def has_next(c):
            return not isinstance(c, int) or c < CHUNKS - 1

        def hidden_tile(j):
            if isinstance(j, int):
                return hidden[:, j, :]
            return hidden[:, bass.ds(j, 1), :].rearrange("p o d -> p (o d)")

        def fills_upto(G, parity):
            if isinstance(G, int):
                return (G // 2 + 1) * FILLS if G >= 0 else 0
            return (G - parity) * (FILLS // 2) + FILLS

        def column(v):
            return v.rearrange("(k p) -> p k", p=P)

        block = ctx.enter_context(nc.Block())

        @block.sync
        def _(sp):
            def address_follows():
                sp.wait_ge(s["pool_consts"], 1)

            def load_x(b):
                if not isinstance(b, int) or b > 0:
                    wait(sp, "x_loaded", b * 16)
                    address_follows()
                sp.dma_start(hidden[:, bass.ds(b * TT, TT), :] if not isinstance(b, int) else hidden[:, b * TT:(b + 1) * TT, :],
                             token_rows(x, b)).then_inc(s["x_loaded"], 16)

            def load_ctx(b):
                if not isinstance(b, int) or b > 0:
                    wait(sp, "ctx_tr", b * 2)
                    address_follows()
                sp.dma_start(ctx_sb[:, :, :], token_rows(ctx_in, b)).then_inc(s["ctx_loaded"], 16)

            def token_rows(src, b):
                rows = src[b:b + 1] if isinstance(b, int) else src[bass.ds(b, 1)]
                return rows.rearrange("o (t p) d -> p (o t) d", p=P)

            def load_small(dst, src, sem):
                with nc.allow_non_contiguous_dma(reason="per-partition vectors, a few KB"):
                    sp.dma_start(dst, src).then_inc(s[sem], 16)

            def load_qk_piece(c):
                for n, w in ((0, q_w), (1, k_w)):
                    sp.dma_start(w_att_raw[:, n, 1, :, c * P:(c + 1) * P],
                                 w[:, c * P:(c + 1) * P].rearrange("(k p) n -> p k n", p=P)).then_inc(wqk_loaded[c], 16)

            load_x(0)
            load_small(cols[:, LN1W:LN1W + KT], column(ln1_w), "ln1_loaded")
            load_small(cols[:, LN1B:LN1B + KT], column(ln1_b), "ln1_loaded")
            load_ctx(0)
            load_qk_piece(0)
            load_small(mrow_raw[:, :], mask, "maskrow_loaded")
            load_small(cols[:, QB:QB + KT], column(q_b), "qkb_loaded")
            load_small(cols[:, KB_:KB_ + KT], column(k_b), "qkb_loaded")
            sp.dma_start(w_att_raw[:, 2, 1, :, :], v_w.rearrange("(k p) n -> p k n", p=P)).then_inc(s["wv_loaded"], 16)
            for c in range(1, NG):
                load_qk_piece(c)
            load_small(maskcol_raw[:, :], mask.rearrange("b (c p) -> p (b c)", p=P), "maskcol_loaded")
            sp.dma_start(w_att_raw[:, 3, 1, :, :], c_w.rearrange("(k p) n -> p k n", p=P)).then_inc(s["wc_loaded"], 16)
            load_x(1)
            sp.wait_ge(s["mask_ready"], 1)
            sp.wait_ge(s["pool_consts"], 5)
            sp.dma_start(mask_rows, maskrow[:, :, :]).then_inc(s["mask_stored"], 16)
            sp.wait_ge(s["mask_stored"], 16)

            def step(it, g):
                G = it * NG + g + 3
                b = it if g == 0 else it + 1
                if g == 0 and batch(it + 2) and not (isinstance(it, int) and it == -1):
                    load_x(it + 2)
                if g == 1 and batch(it + 2):
                    load_ctx(it + 2)
                if group(G):
                    scratch_rows = qk_rows[(g + 3) % 2]
                    filled = stack_filled[(g + 3) % 2]
                    wait(sp, filled, fills_upto(G - 2, (g + 3) % 2))
                    address_follows()
                    wait(sp, "qk_lo_done", (G + 1) * 2)
                    sp.dma_start(scratch_rows.rearrange("d h n q -> h d n q"), qk[:, :, :].bitcast(fp32)).then_inc(s["qk_stored"], 16)
                if group(G - 2):
                    slot = slice(GH * ((g + 1) % NG), GH * ((g + 1) % NG) + GH)
                    address_follows()
                    wait(sp, "mrow_ready", G - 1)
                    sp.dma_start(qst[3 * HD:3 * HD + 3, slot, :].bitcast(fp32),
                                 mrow[:, :].bitcast(fp32)).then_inc(s["m_stored"], 16)
                if group(G):
                    slot = slice(GH * ((g + 3) % NG), GH * ((g + 3) % NG) + GH)
                    row = mask_rows[b:b + 1] if isinstance(b, int) else mask_rows[bass.ds(b, 1)]
                    sp.dma_start(stacks[3 * HD:3 * HD + 1, slot, :, :].bitcast(fp32),
                                 row.rearrange("b (o n) q -> b o n q", o=1).to_broadcast([1, GH, 2, LK])).then_inc(filled, 16)
                    address_follows()
                    wait(sp, "qk_stored", (G + 1) * 16)
                    for r, parts in enumerate((slice(1, 3), slice(1, 4, 2), slice(0, 3, 2))):
                        sp.dma_start(stacks[HD * r:HD * r + HD, slot, :, :].bitcast(fp32),
                                     scratch_rows[:, :, parts, :]).then_inc(filled, 16)

            def load_tile(i):
                sp.dma_start(w_mlp_raw[i][:, 1, :].rearrange("p (k f) -> p k f", k=KT),
                             fc_w[:, i * P:(i + 1) * P].rearrange("(k p) f -> p k f", p=P)).then_inc(w2_loaded[i], 16)
                sp.dma_start(w_mlp_raw[i][:, 3, :], proj_w[i * P:(i + 1) * P, :]).then_inc(w2_loaded[i], 16)

            def tail(it, g):
                if it == B - 1 and g == 0:
                    wait(sp, "qk_proj", GROUPS)
                    wait(sp, "v_proj", B * 2)
                if it == B - 1 and g < 3:
                    load_tile(2 * g)
                    load_tile(2 * g + 1)

            iterations(sp, step, tail=tail)

            wait(sp, "c_proj", B * 2)
            sp.dma_start(pb_bc[:, :], proj_b.rearrange("(o n) -> o n", o=1).to_broadcast([P, D])).then_inc(s["pb_loaded"], 16)
            for i in range(6, FT):
                load_tile(i)

            def store(c, first):
                for t in range(CH):
                    wait(sp, "out_added", c * CH + (t + 1))
                    address_follows()
                    rows = out_rows(c * CH + t)
                    src = hidden[:, c * CH + t, :] if isinstance(c, int) else hidden[:, bass.ds(c * CH + t, 1), :].rearrange("p o d -> p (o d)")
                    sp.dma_start(rows, src).then_inc(s["out_stored"], 16)

            def out_rows(j):
                flat = out.rearrange("b (t p) d -> (b t) p d", p=P)
                return flat[j] if isinstance(j, int) else flat[bass.ds(j, 1)].rearrange("o p d -> (o p) d")

            chunks(sp, store)
            sp.wait_ge(s["out_stored"], 16 * B * TT)

        @block.gpsimd
        def _(pool):
            def small(dst, src, sem):
                with nc.allow_non_contiguous_dma(reason="per-partition vectors, a few KB"):
                    pool.dma_start(dst, src).then_inc(s[sem], 16)

            def repeated(v):
                return v.rearrange("(o n) -> o n", o=1).to_broadcast([P, D])

            pool.memset(ident[:, :], 0.0).then_inc(s["ident_zero"], 1)
            pool.wait_ge(s["ident_zero"], 1)
            pool.affine_select(out=ident[:, :], in_=ident[:, :], compare_op=ALU.not_equal, fill=1.0,
                               base=0, pattern=[[-1, P]], channel_multiplier=1).then_inc(s["ident_ready"], 1)
            pool.memset(mhalf[:, :], -0.5).then_inc(s["pool_consts"], 1)
            pool.wait_ge(s["pool_consts"], 1)

            def inverse_std(b, n, var_sem, out_sem):
                wait(pool, var_sem, b + 1)
                pool.tensor_tensor(rstd[:, 0:n], vareps[:, 0:n], mhalf[:, 0:n], ALU.pow).then_inc(s[out_sem], 1)

            def constants():
                pool.memset(m12[:, :, :].bitcast(fp32), 0.0).then_inc(s["pool_consts"], 1)
                pool.memset(vparts[:, :, :, 0:1], 1.0).then_inc(s["pool_consts"], 1)
                pool.memset(maskrow[:, 0, :], 1.0).then_inc(s["pool_consts"], 1)
                pool.wait_ge(s["pool_consts"], 4)
                pool.memset(kst[3 * HD:3 * HD + 3, :, :].bitcast(fp32), 1.0).then_inc(s["pool_consts"], 1)
                pool.wait_ge(s["pool_consts"], 5)
                small(vb_bc[:, :], repeated(v_b), "small_loaded")
                small(cb_bc[:, :], repeated(c_b), "small_loaded")
                split_weight_lo(3)
                for dst, src in ((cols[:, LN2W:LN2W + KT], ln2_w), (cols[:, LN2B:LN2B + KT], ln2_b),
                                 (cols[:, FCB:FCB + FT], fc_b)):
                    small(dst, column(src), "mlp_columns_loaded")

            def split_weight_lo(n):
                pool.wait_ge(s["w_hi_act"], n - 1)
                pool.tensor_tensor(w_att[:, n, 1, :, :], w_att_raw[:, n, 1, :, :], w_att[:, n, 0, :, :].bitcast(fp32),
                                   ALU.subtract).then_inc(s["w_lo_pool"], 1)

            def step(it, g):
                G = it * NG + g
                for u in range(4):
                    if u == 2 and g == 2 and batch(it + 2):
                        inverse_std(it + 2, TT, "ln_var", "ln_rstd")
                    if u == 2 and g == 0 and batch(it - 1):
                        b = it - 1
                        wait(pool, "pv_taken", (b + 1) * 16)
                        for t in range(TT):
                            a = att[:, t, :].rearrange("p (h d) -> p h d", h=H)
                            pool.tensor_tensor(a, a, rl[:, t, :].rearrange("p (h o) -> p h o", o=1).to_broadcast([P, H, HD]),
                                               ALU.mult).then_inc(s["att_normed"], 1)
                    if group(G):
                        wait(pool, "p_hi_done", (G * 4) + (u + 1))
                        wait(pool, "pv_mm", (G - 1) * 2)
                        slot = (g % 2) * 4 + u
                        pool.tensor_tensor(p_lo[:, slot, :], p32[:, u % 2, :], p_hi[:, slot, :],
                                           ALU.subtract).then_inc(s["p_lo_done"], 1)
                if g == 1 and batch(it + 1):
                    b = it + 1
                    wait(pool, "x_normed", (b + 1) * 2)
                    wait(pool, "small_loaded", SMALL)
                    for t in range(TT):
                        h = hidden_tile(b * TT + t)
                        pool.tensor_tensor(h, h, cb_bc[:, :], ALU.add).then_inc(s["cb_added"], 1)

            def ln2(j):
                inverse_std(j, 1, "y_var", "y_rstd")

            def tail(it, g):
                if (it, g) == (B - 2, 3):
                    ln2(0)
                if it == B - 1 and g < 3:
                    ln2(g + 1)

            iterations(pool, step, weights=constants, tail=tail)

            def pb(j):
                wait(pool, "y_normed", j + 1)
                h = hidden_tile(j)
                pool.tensor_tensor(h, h, pb_bc[:, :], ALU.add).then_inc(s["pb_added"], 1)

            pool.wait_ge(s["pb_loaded"], 16)
            for t in range(CH):
                pb(t)

            def body(c, first):
                if has_next(c):
                    for t in range(CH):
                        ln2(c * CH + (CH + t))
                        pb(c * CH + (CH + t))

            chunks(pool, body)

        @block.scalar
        def _(act):
            act.wait_ge(s["ident_ready"], 1)
            act.activation(act_scratch[:, :], ident[:, 0:1], ACT.Exp)

            def qk_weights_hi(c):
                act.wait_ge(wqk_loaded[c], 32)
                for n in range(2):
                    act.activation(w_att[:, n, 0, :, c * P:(c + 1) * P], w_att_raw[:, n, 1, :, c * P:(c + 1) * P],
                                   ACT.Copy).then_inc(s["w_hi_qk"], 1)

            def weights_hi(n, sem):
                act.wait_ge(s[sem], 16)
                act.activation(w_att[:, n, 0, :, :], w_att_raw[:, n, 1, :, :], ACT.Copy).then_inc(s["w_hi_act"], 1)

            qk_weights_hi(0)

            def weights():
                weights_hi(2, "wv_loaded")
                for c in range(1, NG):
                    qk_weights_hi(c)
                act.wait_ge(s["qkb_loaded"], 32)

            def exps(it, g, u):
                G = it * NG + g
                if not group(G):
                    return
                kc = u % KC
                n = G * 4 + u
                wait(act, "st_mm", n + 1)
                wait(act, "p_lo_done", n - 1)
                act.activation(p32[:, u % 2, :], psum[:, ST + kc, :], ACT.Exp, bias=maskbias[:, kc:kc + 1], scale=SCALE32)
                wait(act, "pv_mm", (G - 1) * 2)
                act.activation(p_hi[:, (g % 2) * 4 + u, :], psum[:, ST + kc, :], ACT.Exp, bias=maskbias[:, kc:kc + 1],
                               scale=SCALE32).then_inc(s["p_hi_done"], 1)

            def context_hi(it, j):
                b = it + 1
                wait(act, "ctx_tr", b * 2 + (j + 1))
                act.activation(cs[:, 0, 2 * j:2 * j + 2, :], in_bank("ctx", j).rearrange("p (k q) -> p k q", k=2),
                               ACT.Copy).then_inc(s["ctx_hi_done"], 1)

            def first_part(b):
                wait(act, "mask_stored", 16)
                wait(act, "v_rest", b)
                wait(act, "v_cast", b * 2)
                wait(act, "v_added", (b + 1) * 2)
                act.activation(v1[:, :, :], v32[:, :, :], ACT.Copy).then_inc(s["v1_cast"], 1)

            def values_cast(b, part):
                wait(act, "v_rest", b + 1)
                wait(act, "pv_mm", b * 8)
                lo = 1 + HD * part
                act.activation(vparts[:, :, :, lo:lo + HD], (v32 if part else v1)[:, :, :].rearrange("p c (h d) -> p c h d", h=H),
                               ACT.Copy).then_inc(s["v_cast"], 1)

            def qk_high(it, g):
                G = it * NG + g + 3
                if group(G):
                    wait(act, "qk_proj", G + 1)
                    wait(act, "qk_stored", G * 16)
                    for n, col in ((0, QB), (1, KB_)):
                        act.activation(qk[:, 1 + n, :], in_bank("qk", g)[:, n * LQ:(n + 1) * LQ], ACT.Identity,
                                       bias=cols[:, col + (g + 3) % NG:col + (g + 3) % NG + 1]).then_inc(s["qk_hi_done"], 1)

            def maxima_out(it, g):
                G = it * NG + g + 1
                if group(G):
                    wait(act, "m_tr", G + 1)
                    wait(act, "m_stored", G * 16)
                    act.activation(mrow[:, :], in_bank("m", g)[0:3 * GH, 0:LQ], ACT.Copy).then_inc(s["mrow_ready"], 1)

            def attention_hi(b):
                wait(act, "c_proj", b * 2)
                for j in range(2):
                    wait(act, "att_tr", b * 2 + (j + 1))
                    act.activation(att_t[:, 0, 2 * j:2 * j + 2, :], in_bank("att", j).rearrange("p (k q) -> p k q", k=2),
                                   ACT.Copy).then_inc(s["att_hi_done"], 1)

            def x_hi(b):
                wait(act, "x_affine_act", (b + 1) * 2)
                wait(act, "x_affine_dve", (b + 1) * 2)
                act.activation(xs[:, 0, :, :], x_t[:, :, :], ACT.Copy).then_inc(s["x_hi_done"], 1)

            def affine_x(b):
                if isinstance(b, int) and b == 0:
                    act.wait_ge(s["ln1_loaded"], 32)
                wait(act, "x_tr", b * 2 + 1)
                wait(act, "x_hi_done", b)
                wait(act, "x_lo_done", b)
                for k in range(2):
                    act.activation(x_t[:, k, :], in_bank("x", 0)[:, k * LQ:(k + 1) * LQ], ACT.Identity,
                                   scale=cols[:, LN1W + k:LN1W + k + 1],
                                   bias=cols[:, LN1B + k:LN1B + k + 1]).then_inc(s["x_affine_act"], 1)

            def mask_columns(b):
                wait(act, "p_hi_done", b * 16)
                cut = slice(b * KC, (b + 1) * KC) if isinstance(b, int) else bass.ds(b * KC, KC)
                act.activation(maskbias[:, :], maskcol[:, cut], ACT.Copy).then_inc(s["maskbias_ready"], 1)

            def step(it, g):
                if g == 0 and batch(it):
                    wait(act, "maskbias_ready", it + 1)
                qk_high(it, g)
                if isinstance(it, int) and (it, g) == (-1, 1):
                    weights_hi(3, "wc_loaded")
                    act.wait_ge(s["mask_ready"], 3)
                    mask_columns(0)
                if isinstance(it, int) and (it, g) == (-1, 0):
                    x_hi(0)
                if g == 0:
                    if batch(it + 1):
                        context_hi(it, 0)
                    exps(it, g, 0)
                    if batch(it + 1):
                        context_hi(it, 1)
                    exps(it, g, 1)
                    maxima_out(it, g)
                    if batch(it + 1) and not (isinstance(it, int) and it == -1):
                        x_hi(it + 1)
                    if batch(it):
                        values_cast(it, 1)
                if g == 1:
                    exps(it, g, 0)
                    maxima_out(it, g)
                    if batch(it - 1):
                        attention_hi(it - 1)
                    exps(it, g, 1)
                if g >= 2:
                    exps(it, g, 0)
                    exps(it, g, 1)
                    maxima_out(it, g)
                if g == 3 and batch(it + 2):
                    affine_x(it + 2)
                exps(it, g, 2)
                exps(it, g, 3)
                if g == 0 and batch(it):
                    values_cast(it, 0)
                if g == 2 and batch(it + 1):
                    first_part(it + 1)
                if g == 3 and batch(it + 1) and not (isinstance(it, int) and it == -1):
                    mask_columns(it + 1)

            def affine(c, j, t):
                wait(act, "y_tr", j + 1)
                wait(act, "y_lo_done", (j - t))
                for k in range(KT):
                    act.activation(y_t[:, k, t * P:(t + 1) * P], turned(c, t)[:, k * P:(k + 1) * P], ACT.Identity,
                                   scale=cols[:, LN2W + k:LN2W + k + 1],
                                   bias=cols[:, LN2B + k:LN2B + k + 1]).then_inc(s["y_affine"], 1)

            def gelu(F, f):
                wait(act, "fc_mm", F + 1)
                wait(act, "h_lo_done", F - 1)
                act.activation(h32[:, f % 2, :], psum[:, FC + f % 2, :], ACT.Gelu_apprx_tanh,
                               bias=cols[:, FCB + f:FCB + f + 1]).then_inc(s["h_done"], 1)

            def tail(it, g):
                if (it, g) == (B - 1, 2):
                    act.wait_ge(s["mlp_columns_loaded"], 3 * 16)
                    wait(act, "x_lo_done", B)
                    wait(act, "qk_stored", GROUPS * 16)
                if it == B - 1 and g >= 2:
                    for t in (2 * g - 4, 2 * g - 3):
                        affine(0, t, t)
                if it == B and g == 1:
                    wait(act, "v_split", B)
                    gelu(0, 0)

            iterations(act, step, weights=weights, tail=tail)

            def body(c, first):
                for i in range(FT):
                    if i < FT - 1:
                        gelu(c * FT + (i + 1), i + 1)
                    elif has_next(c):
                        gelu(c * FT + FT, 0)
                    if has_next(c) and i % 3 == 0 and 3 <= i <= 12:
                        t = i // 3 - 1
                        affine(c + 1, c * CH + (CH + t), t)

            chunks(act, body)

        @block.vector
        def _(dve):
            def qk_weights_lo(c):
                for n in range(2):
                    dve.wait_ge(s["w_hi_qk"], 2 * c + n + 1)
                    piece = w_att[:, n, :, :, c * P:(c + 1) * P]
                    dve.tensor_tensor(piece[:, 1], w_att_raw[:, n, 1, :, c * P:(c + 1) * P], piece[:, 0].bitcast(fp32),
                                      ALU.subtract).then_inc(s["w_lo_dve"], 1)

            def first_weights_lo():
                qk_weights_lo(0)
                dve.wait_ge(s["maskrow_loaded"], 16)
                dve.tensor_scalar(maskrow[:, 1, :], mrow_raw[:, :], MASKED, -MASKED, ALU.mult, ALU.add).then_inc(s["mask_ready"], 1)

            def weights_lo():
                dve.wait_ge(s["w_hi_act"], 1)
                dve.tensor_tensor(w_att[:, 2, 1, :, :], w_att_raw[:, 2, 1, :, :], w_att[:, 2, 0, :, :].bitcast(fp32),
                                  ALU.subtract).then_inc(s["w_lo_v"], 1)
                for c in range(1, NG):
                    qk_weights_lo(c)

            def mask_columns():
                dve.wait_ge(s["small_loaded"], SMALL)
                dve.wait_ge(s["maskcol_loaded"], 16)
                dve.tensor_scalar(maskcol[:, :], maskcol_raw[:, :], SCALE32 * MASKED, -SCALE32 * MASKED,
                                  ALU.mult, ALU.add).then_inc(s["mask_ready"], 1)
                dve.wait_ge(s["mask_ready"], 2)
                dve.tensor_scalar_add(maskcol[:, :], maskcol[:, :], PSHIFT).then_inc(s["mask_ready"], 1)

            def maximum(it, g, heads):
                G = it * NG + g + 2
                if not group(G):
                    return
                if heads[0] == 0:
                    wait(dve, "m_lo_done", G)
                for h in heads:
                    n = G * 4 + h
                    wait(dve, "max_mm", n + 1)
                    dve.tensor_reduce(out=negm[:, :, h:h + 1], in_=psum[:, MX + h % 2, :].rearrange("p (t k) -> p t k", t=TT),
                                      axis=AX.X, op=ALU.max, negate=True).then_inc(s["max_taken"], 1)
                if heads[-1] == GH - 1:
                    wait(dve, "max_taken", (G + 1) * 4)
                    wait(dve, "m_tr", G)
                    dve.tensor_copy(m12[:, :, GH:2 * GH], negm[:, :, :]).then_inc(s["m_hi_done"], 1)
                    wait(dve, "m_hi_done", G + 1)
                    dve.tensor_tensor(m12[:, :, 2 * GH:3 * GH], negm[:, :, :], m12[:, :, GH:2 * GH].bitcast(fp32),
                                      ALU.subtract).then_inc(s["m_lo_done"], 1)

            def statistics(b, tiles, stats_sem, mv_sem, var_sem):
                n = len(tiles)
                for t, j in enumerate(tiles):
                    dve.bn_stats(stats[:, t, :], hidden_tile(j)).then_inc(s[stats_sem], 1)
                wait(dve, stats_sem, (b + 1) * n)
                dve.memset(scratch[:, :], 0.0)
                for t in range(n):
                    dve.bn_aggr(mv[:, t, :], stats[:, t, :]).then_inc(s[mv_sem], 1)
                wait(dve, mv_sem, (b + 1) * n)
                dve.tensor_scalar_add(vareps[:, 0:n], mv[:, 0:n, 1], EPS).then_inc(s[var_sem], 1)

            def add_hidden(it, t):
                b = it - 1 - t
                wait(dve, "c_proj", b * 2 + (t + 1))
                wait(dve, "cb_added", (b + 1) * 2)
                h = hidden_tile(b * TT + t)
                dve.tensor_tensor(h, in_bank("c", t), h, ALU.add).then_inc(s["hidden_added"], 1)

            def add_values(it, t):
                b = it + 1
                wait(dve, "v_proj", b * 2 + (t + 1))
                wait(dve, "v_split", b)
                dve.tensor_tensor(v32[:, t, :], in_bank("v", t), vb_bc[:, :], ALU.add).then_inc(s["v_added"], 1)

            def low_parts(it, g):
                G = it * NG + g + 3
                if group(G):
                    wait(dve, "qk_hi_done", (G + 1) * 2)
                    for n, col in ((0, QB), (1, KB_)):
                        piece = slice(n * LQ, (n + 1) * LQ)
                        dve.scalar_tensor_tensor(out=qk[:, 3 * n, :], in0=in_bank("qk", g)[:, piece],
                                                 scalar=cols[:, col + (g + 3) % NG:col + (g + 3) % NG + 1],
                                                 in1=qk[:, 1 + n, :].bitcast(fp32), op0=ALU.add,
                                                 op1=ALU.subtract).then_inc(s["qk_lo_done"], 1)

            v_heads = v32[:, :, :].rearrange("p c (h d) -> p c h d", h=H)

            def affine_x(b):
                if isinstance(b, int) and b == 0:
                    dve.wait_ge(s["ln1_loaded"], 32)
                wait(dve, "x_tr", (b + 1) * 2)
                wait(dve, "x_hi_done", b)
                wait(dve, "x_lo_done", b)
                for k in range(2):
                    dve.tensor_scalar(x_t[:, 2 + k, :], in_bank("x", 1)[:, k * LQ:(k + 1) * LQ],
                                      cols[:, LN1W + 2 + k:LN1W + 3 + k], cols[:, LN1B + 2 + k:LN1B + 3 + k],
                                      ALU.mult, ALU.add).then_inc(s["x_affine_dve"], 1)

            def x_lo(b):
                wait(dve, "x_hi_done", b + 1)
                dve.tensor_tensor(xs[:, 1, :, :], x_t[:, :, :], xs[:, 0, :, :].bitcast(fp32),
                                  ALU.subtract).then_inc(s["x_lo_done"], 1)

            def context_lo(it, j):
                b = it + 1
                wait(dve, "ctx_hi_done", b * 2 + (j + 1))
                dve.tensor_tensor(cs[:, 1, 2 * j:2 * j + 2, :], in_bank("ctx", j).rearrange("p (k q) -> p k q", k=2),
                                  cs[:, 0, 2 * j:2 * j + 2, :].bitcast(fp32), ALU.subtract).then_inc(s["ctx_lo_done"], 1)

            def products_out(it, g):
                G = it * NG + g - 1
                if not group(G):
                    return
                if (g - 1) % NG == 0:
                    wait(dve, "att_tr", it * 2)
                for t in range(TT):
                    wait(dve, "pv_mm", G * 2 + (t + 1))
                    rows = psum[:, PV + t, 0:GH * VW].rearrange("p (h c) -> p h c", c=VW)
                    h0 = GH * ((g - 1) % NG)
                    dve.tensor_reduce(out=att[:, t, h0 * HD:(h0 + GH) * HD].rearrange("p (h d) -> p h d", h=GH),
                                      in_=rows[:, :, 1:VW].rearrange("p h (s d) -> p h d s", s=3),
                                      axis=AX.X, op=ALU.add).then_inc(s["pv_taken"], 1)
                    dve.reciprocal(rl[:, t, h0:h0 + GH], rows[:, :, 0]).then_inc(s["pv_taken"], 1)

            def step(it, g):
                low_parts(it, g)
                if isinstance(it, int) and (it, g) == (-1, 1):
                    mask_columns()
                if isinstance(it, int) and (it, g) == (-1, 0):
                    x_lo(0)
                if g == 0 and batch(it + 1):
                    context_lo(it, 0)
                    context_lo(it, 1)
                if g == 3 and batch(it + 2):
                    b = it + 2
                    wait(dve, "ln_rstd", b + 1)
                    wait(dve, "x_tr", b * 2)
                    wait(dve, "x_hi_done", b)
                    wait(dve, "x_lo_done", b)
                    for t in range(TT):
                        dve.tensor_scalar(xn[:, :, t, :], hidden_tile(b * TT + t).rearrange("p (j d) -> p j d", j=2), mv[:, t, 0:1], rstd[:, t:t + 1],
                                          ALU.subtract, ALU.mult).then_inc(s["x_normed"], 1)
                if isinstance(it, int) and (it, g) == (B - 1, 3):
                    ln2_norm(3, 3)
                if g != 1:
                    products_out(it, g)
                maximum(it, g, (0, 1))
                if g == 0 and batch(it + 1) and not (isinstance(it, int) and it == -1):
                    x_lo(it + 1)
                if g == 0 and batch(it):
                    wait(dve, "v_cast", it * 2 + 1)
                    for kc in range(KC):
                        ins = dve.tensor_tensor(vparts[:, kc, :, 1 + 2 * HD:VW], v_heads[:, kc],
                                                vparts[:, kc, :, 1 + HD:1 + 2 * HD], ALU.subtract)
                    ins.then_inc(s["v_split"], 1)
                if g == 1 and batch(it - 1):
                    b = it - 1
                    for j in range(2):
                        wait(dve, "att_hi_done", b * 2 + (j + 1))
                        dve.tensor_tensor(att_t[:, 1, 2 * j:2 * j + 2, :], in_bank("att", j).rearrange("p (k q) -> p k q", k=2),
                                          att_t[:, 0, 2 * j:2 * j + 2, :].bitcast(fp32), ALU.subtract).then_inc(s["att_lo_done"], 1)
                if g == 1:
                    products_out(it, g)
                if g == 2 and batch(it + 2):
                    b = it + 2
                    wait(dve, "x_loaded", (b + 1) * 16)
                    wait(dve, "ln_rstd", b)
                    wait(dve, "x_normed", b * 2)
                    statistics(b, [b * TT + t for t in range(TT)], "ln_stats", "ln_mv", "ln_var")
                if g in (1, 2) and batch(it + 1):
                    add_values(it, g - 1)
                last = isinstance(it, int) and (it, g) == (B - 1, 0)
                if last:
                    maximum(it, g, (2, 3))
                if g == 0 and batch(it - 2):
                    add_hidden(it, 1)
                if isinstance(it, int) and (it, g) == (B - 1, 3):
                    weights(1)
                    split_y(0)
                if g == 3 and batch(it - 1):
                    add_hidden(it, 0)
                if g == 3 and batch(it + 2):
                    affine_x(it + 2)
                if not last:
                    maximum(it, g, (2, 3))
                if g == 3 and batch(it + 1):
                    wait(dve, "v1_cast", it + 2)
                    dve.tensor_tensor(v32[:, :, :], v32[:, :, :], v1[:, :, :], ALU.subtract).then_inc(s["v_rest"], 1)

            def weights(i):
                dve.wait_ge(w2_loaded[i], 32)
                dve.tensor_copy(w_mlp[i][:, 0::2, :], w_mlp_raw[i][:, 1::2, :]).then_inc(s["w2_hi"], 1)
                dve.wait_ge(s["w2_hi"], i + 1)
                dve.tensor_tensor(w_mlp[i][:, 1::2, :], w_mlp_raw[i][:, 1::2, :], w_mlp[i][:, 0::2, :].bitcast(fp32),
                                  ALU.subtract).then_inc(s["w2_lo"], 1)

            def ln2_stats(j):
                wait(dve, "y_rstd", j)
                wait(dve, "y_normed", j)
                statistics(j, [j], "y_stats", "y_mv", "y_var")

            def ln2_norm(j, t):
                wait(dve, "y_rstd", j + 1)
                wait(dve, "y_tr", j - 1)
                dve.tensor_scalar(yn[:, t % 2, :], hidden_tile(j), mv[:, 0, 0:1], rstd[:, 0:1],
                                  ALU.subtract, ALU.mult).then_inc(s["y_normed"], 1)

            def split_y(c):
                wait(dve, "y_affine", (c + 1) * CH * KT)
                wait(dve, "fc_mm", c * FT)
                for k in range(KT):
                    dve.tensor_copy(y_hi[:, k, :], y_t[:, k, :]).then_inc(s["y_hi_done"], 1)
                    wait(dve, "y_hi_done", c * KT + (k + 1))
                    dve.tensor_tensor(y_lo[:, k, :], y_t[:, k, :], y_hi[:, k, :].bitcast(fp32),
                                      ALU.subtract).then_inc(s["y_lo_done"], 1)

            def split_h(F, f):
                wait(dve, "h_done", F + 1)
                wait(dve, "proj_mm", (F - 1) * CH)
                dve.tensor_copy(h_hi[:, f % 2, :], h32[:, f % 2, :]).then_inc(s["h_hi_done"], 1)
                wait(dve, "h_hi_done", F + 1)
                dve.tensor_tensor(h_lo[:, f % 2, :], h32[:, f % 2, :], h_hi[:, f % 2, :].bitcast(fp32),
                                  ALU.subtract).then_inc(s["h_lo_done"], 1)

            def tail(it, g):
                if (it, g) == (B - 2, 3):
                    wait(dve, "hidden_added", CH)
                    wait(dve, "ln_rstd", B)
                    wait(dve, "x_normed", B * 2)
                    ln2_stats(0)
                if it == B - 1:
                    if g < 3:
                        ln2_norm(g, g)
                    if g < 3:
                        ln2_stats(g + 1)
                    if g == 2:
                        weights(0)
                if (it, g) == (B, 1):
                    weights(2)
                    wait(dve, "att_tr", B * 2)
                    split_h(0, 0)
                    weights(3)

            iterations(dve, step, first_weights_lo, weights_lo, tail)

            def add_out(c):
                for t in range(CH):
                    wait(dve, "proj_mm", (c + 1) * FT * CH - CH + (t + 1))
                    wait(dve, "pb_added", c * CH + (t + 1))
                    h = hidden_tile(c * CH + t)
                    dve.tensor_tensor(h, psum[:, ACC[t], :], h, ALU.add).then_inc(s["out_added"], 1)

            wait(dve, "hidden_added", B * 2)

            def body(c, first):
                for i in range(FT):
                    if first and i + 4 < FT:
                        weights(i + 4)
                    if i < FT - 1:
                        split_h(c * FT + (i + 1), i + 1)
                    elif has_next(c):
                        split_y(c + 1)
                        add_out(c)
                        split_h(c * FT + FT, 0)
                    if has_next(c):
                        for t in range(CH):
                            if i == 3 * t + 1:
                                ln2_stats(c * CH + (CH + t))
                            if i == 3 * t + 2:
                                ln2_norm(c * CH + (CH + t), t)

            chunks(dve, body)
            add_out(CHUNKS - 1)

        @block.tensor
        def _(pe):
            def three_passes(out_ap, pairs):
                n = len(pairs)
                for i, (a_hi, a_lo, b_hi, b_lo) in enumerate(pairs):
                    nc.tensor.matmul(out_ap, a_hi, b_hi, start=(i == 0), stop=False)
                    nc.tensor.matmul(out_ap, a_hi, b_lo, start=False, stop=False)
                    ins = nc.tensor.matmul(out_ap, a_lo, b_hi, start=False, stop=(i == n - 1))
                return ins

            pe.wait_ge(s["ident_ready"], 1)

            def transposed_scores(it, g, pair):
                G = it * NG + g
                if not group(G):
                    return
                if pair == 0:
                    wait(pe, "m_stored", (G + 1) * 16)
                for kc in range(KC):
                    n = G * 4 + 2 * pair + kc
                    wait(pe, "p_hi_done", n - 1)
                    for hh in range(2):
                        h = GH * g + 2 * pair + hh
                        ins = nc.tensor.matmul(psum[:, ST + kc, hh * LQ:(hh + 1) * LQ],
                                               kst[0:SUBROWS, h, kc * P:(kc + 1) * P], qst[0:SUBROWS, h, :],
                                               start=True, stop=True)
                    ins.then_inc(s["st_mm"], 1)

            def scores(it, g, heads):
                G = it * NG + g + 2
                if not group(G):
                    return
                if heads[0] == 0:
                    wait(pe, stack_filled[g % 2], fills_upto(G, g % 2))
                    wait(pe, "pool_consts", 5)
                for hh in heads:
                    h = GH * ((g + 2) % NG) + hh
                    wait(pe, "max_taken", G * 4 + (hh - 1))
                    for t in range(TT):
                        ins = nc.tensor.matmul(psum[:, MX + hh % 2, t * LK:(t + 1) * LK],
                                               qst[0:MAXROWS, h, t * P:(t + 1) * P], kst[0:MAXROWS, h, :],
                                               start=True, stop=True)
                    ins.then_inc(s["max_mm"], 1)

            def project_qk(it, g):
                G = it * NG + g + 3
                if not group(G):
                    return
                b = it if g == 0 else it + 1
                wait(pe, "ctx_lo_done", (b + 1) * 2)
                wait(pe, "x_lo_done", b + 1)
                if isinstance(it, int) and it == -1:
                    pe.wait_ge(s["w_lo_dve"], 2 * G + 2)
                elif isinstance(it, int) and it == 0 and g == 0:
                    pe.wait_ge(s["w_lo_dve"], 2 * NG)
                bank = bank_of(it, "qk", g)
                c0 = P * ((g + 3) % NG)
                for n, src in ((0, xs), (1, cs)):
                    ins = three_passes(bank[:, n * LQ:(n + 1) * LQ],
                                       [(w_att[:, n, 0, k, c0:c0 + P], w_att[:, n, 1, k, c0:c0 + P],
                                         src[:, 0, k, :], src[:, 1, k, :]) for k in range(KT)])
                ins.then_inc(s["qk_proj"], 1)

            def project_v(it, t):
                if not batch(it + 1):
                    return
                wait(pe, "w_lo_v", 1)
                bank = bank_of(it, "v", t)
                three_passes(bank, [(cs[:, 0, k, t * P:(t + 1) * P], cs[:, 1, k, t * P:(t + 1) * P],
                                     w_att[:, 2, 0, k, :], w_att[:, 2, 1, k, :]) for k in range(KT)]).then_inc(s["v_proj"], 1)

            def project_c(it, t):
                b = it - 1 - t
                if not batch(b):
                    return
                wait(pe, "att_lo_done", (b + 1) * 2)
                wait(pe, "w_lo_pool", 1)
                bank = bank_of(it, "c", t)
                three_passes(bank, [(att_t[:, 0, k, t * P:(t + 1) * P], att_t[:, 1, k, t * P:(t + 1) * P],
                                     w_att[:, 3, 0, k, :], w_att[:, 3, 1, k, :]) for k in range(KT)]).then_inc(s["c_proj"], 1)

            def transposes(it, kind, j, b, src, ready, per_batch, done):
                if not batch(b):
                    return
                wait(pe, ready, (b + 1) * per_batch)
                bank = bank_of(it, kind, j)
                for i in range(2):
                    for t in range(TT):
                        k = 2 * j + i
                        ins = nc.tensor.transpose(bank[:, i * LQ + t * P:i * LQ + (t + 1) * P],
                                                  src[:, j, t, i * P:(i + 1) * P] if kind == "x" else src[:, t, k * P:(k + 1) * P],
                                                  ident[:, :])
                ins.then_inc(s[done], 1)

            def values(it, g):
                G = it * NG + g - 1
                if not group(G):
                    return
                b = it - 1 if g == 0 else it
                wait(pe, "p_lo_done", (G + 1) * 4)
                wait(pe, "v_split", b + 1)
                wait(pe, "v_cast", (b + 1) * 2)
                gp = (g - 1) % NG
                for t in range(TT):
                    wait(pe, "pv_taken", (G - 1) * 4 + (2 * t + 2))
                    for hh in range(GH):
                        o = psum[:, PV + t, hh * VW:(hh + 1) * VW]
                        for kc in range(KC):
                            slot = (gp % 2) * 4 + (hh // 2) * 2 + kc
                            cut = slice((hh % 2) * LQ + t * P, (hh % 2) * LQ + (t + 1) * P)
                            nc.tensor.matmul(o, p_hi[:, slot, cut], vparts[:, kc, GH * gp + hh, :],
                                             start=(kc == 0), stop=False)
                            ins = nc.tensor.matmul(o[:, 0:VW_LO], p_lo[:, slot, cut], vparts[:, kc, GH * gp + hh, 0:VW_LO],
                                                   start=False, stop=(kc == KC - 1))
                    ins.then_inc(s["pv_mm"], 1)

            def transpose_max(it, g):
                G = it * NG + g + 1
                if not group(G):
                    return
                wait(pe, "m_lo_done", G + 1)
                bank = bank_of(it, "m", g)
                for t in range(TT):
                    ins = nc.tensor.transpose(bank[0:3 * GH, t * P:(t + 1) * P], m12[:, t, :].bitcast(fp32), ident[:, :])
                ins.then_inc(s["m_tr"], 1)

            def step(it, g):
                if isinstance(it, int) and (it, g) == (B, 0):
                    values(it, g)
                    project_c(it, 1)
                    fc(0, 0, 0)
                    return
                last = isinstance(it, int) and it == B - 1
                project_qk(it, g)
                transposed_scores(it, g, 0)
                if g == 0:
                    transposes(it, "ctx", 0, it + 1, ctx_sb, "ctx_loaded", 16, "ctx_tr")
                    values(it, g)
                    transposes(it, "ctx", 1, it + 1, ctx_sb, "ctx_loaded", 16, "ctx_tr")
                    scores(it, g, (0, 1))
                    transpose_max(it, g)
                    if last:
                        transposed_scores(it, g, 1)
                        scores(it, g, (2, 3))
                    project_c(it, 1)
                if g == 1:
                    transpose_max(it, g)
                    scores(it, g, (0, 1))
                    for j in range(2):
                        transposes(it, "att", j, it - 1, att, "att_normed", 2, "att_tr")
                    values(it, g)
                    project_v(it, 0)
                    if isinstance(it, int) and it == B:
                        fc(0, 1, 1)
                if g == 2:
                    transpose_max(it, g)
                    values(it, g)
                    scores(it, g, (0, 1))
                    project_v(it, 1)
                if g == 3:
                    transpose_max(it, g)
                    values(it, g)
                    scores(it, g, (0, 1))
                    if last:
                        transposed_scores(it, g, 1)
                        transpose_y(0, 2, 2)
                        transpose_y(0, 3, 3)
                    project_c(it, 0)
                    transposes(it, "x", 0, it + 2, xn, "x_normed", 2, "x_tr")
                if not (last and g in (0, 3)):
                    transposed_scores(it, g, 1)
                if last and g == 2:
                    wait(pe, "max_taken", GROUPS * 4)
                    transpose_y(0, 0, 0)
                    transpose_y(0, 1, 1)
                if g == 3:
                    transposes(it, "x", 1, it + 2, xn, "x_normed", 2, "x_tr")
                if not (last and g == 0):
                    scores(it, g, (2, 3))

            def fc(c, F, f):
                wait(pe, "w2_lo", f + 1)
                wait(pe, "h_done", F - 1)
                for k in range(KT):
                    wait(pe, "y_lo_done", c * KT + (k + 1))
                    w = w_mlp[f][:, :, k * P:(k + 1) * P]
                    bank = psum[:, FC + f % 2, :]
                    nc.tensor.matmul(bank, w[:, 0, :], y_hi[:, k, :], start=(k == 0), stop=False)
                    nc.tensor.matmul(bank, w[:, 0, :], y_lo[:, k, :], start=False, stop=False)
                    ins = nc.tensor.matmul(bank, w[:, 1, :], y_hi[:, k, :], start=False, stop=(k == KT - 1))
                ins.then_inc(s["fc_mm"], 1)

            def proj(c, F, f):
                wait(pe, "h_lo_done", F + 1)
                if isinstance(F, int) and F == 0:
                    wait(pe, "p_hi_done", GROUPS * 4)
                    wait(pe, "hidden_added", B * 2)
                for t in range(CH):
                    if f == 0:
                        wait(pe, "out_added", (c - 1) * CH + (t + 1))
                    cut = slice(t * P, (t + 1) * P)
                    acc = psum[:, ACC[t], :]
                    nc.tensor.matmul(acc, h_hi[:, f % 2, cut], w_mlp[f][:, 2, :], start=(f == 0), stop=False)
                    nc.tensor.matmul(acc, h_hi[:, f % 2, cut], w_mlp[f][:, 3, :], start=False, stop=False)
                    nc.tensor.matmul(acc, h_lo[:, f % 2, cut], w_mlp[f][:, 2, :], start=False,
                                     stop=(f == FT - 1)).then_inc(s["proj_mm"], 1)

            def transpose_y(c, j, t):
                wait(pe, "y_normed", j + 1)
                wait(pe, "y_affine", (j - 1) * KT)
                for k in range(KT):
                    ins = nc.tensor.transpose(turned(c, t)[:, k * P:(k + 1) * P], yn[:, t % 2, k * P:(k + 1) * P], ident[:, :])
                ins.then_inc(s["y_tr"], 1)

            iterations(pe, step)

            def body(c, first):
                for i in range(FT):
                    if i < FT - 1 and not (first and i == 0):
                        fc(c, c * FT + (i + 1), i + 1)
                    if has_next(c) and i % 3 == 0 and 3 <= i <= 12:
                        t = i // 3 - 1
                        transpose_y(c + 1, c * CH + (CH + t), t)
                    proj(c, c * FT + i, i)
                if has_next(c):
                    fc(c + 1, c * FT + FT, 0)

            chunks(pe, body)


_INS = ["x", "ctx_2048", "mask_BxS2_bf1"] + ["L0_xattn_" + n for n in (
    "ln1_w", "ln1_b", "q_w", "q_b", "k_w", "k_b", "v_w", "v_b", "cproj_w", "cproj_b",
    "ln2_w", "ln2_b", "fc_w", "fc_b", "proj_w", "proj_b")]
_OUTS = [((8, 256, 512), "float32")]


def kernel(**inputs):
    import numpy as _np
    import concourse.bacc as _bacc
    from concourse import mybir as _mybir
    from concourse.bass_utils import run_bass_kernel_spmd as _run

    nc = _bacc.Bacc("TRN2", target_bir_lowering=False, num_devices=1)
    arrays, args = {}, []
    for name in _INS:
        a = _np.ascontiguousarray(inputs[name])
        if a.dtype == _np.bool_:
            a = a.view(_np.uint8)
        arrays[f"in_{name}_dram"] = a
        args.append(nc.dram_tensor(f"in_{name}_dram", a.shape, _mybir.dt.from_np(a.dtype), kind="ExternalInput").ap())
    for i, (shape, dtype) in enumerate(_OUTS):
        dt = _mybir.dt.from_np(_np.dtype(dtype))
        args.append(nc.dram_tensor(f"out_{i}_dram", shape, dt, kind="ExternalOutput").ap())
    xattn_kernel(nc, *args)
    r = _run(nc, [arrays], core_ids=[0])
    got = tuple(r.results[0][f"out_{i}_dram"] for i in range(len(_OUTS)))
    return got[0]
```
